# Optimizing a Trainium2 kernel written in Bass

```python
import numpy as np
import jax
import jax.numpy as jnp

def _softmax(x, axis=-1):
    return jax.nn.softmax(x, axis=axis)

def _gelu(x):
    return jax.nn.gelu(x, approximate=True)

def _silu(x):
    return jax.nn.silu(x)

def _sigmoid(x):
    return jax.nn.sigmoid(x)

def _layernorm(x, axis=-1, eps=1e-05):
    m = jnp.mean(x, axis=axis, keepdims=True)
    v = jnp.var(x, axis=axis, keepdims=True)
    return (x - m) / jnp.sqrt(v + eps)

def _scatter_add(tgt, idx, src, axis=0):
    return tgt.at[idx].add(src)

def _segment_sum(src, seg, n):
    return jax.ops.segment_sum(src, seg, n)
kernel_name = 'mk_gnn_resnorm_d4_gnn_r16_e4ee1d'

def setup_inputs(seed: int=0):
    np.random.seed(seed)
    _w = jnp.asarray

    def _rec_inputs():
        import jax
        import jax.numpy as jnp
        _gk = jax.random.key(seed)
        x = -0.0005121 + 1.001 * jax.random.normal(jax.random.fold_in(_gk, 1), (6250, 64), jnp.float32)
        src = jax.random.randint(jax.random.fold_in(_gk, 2), (200000,), 0, 6250, jnp.int32)
        dst = jnp.minimum((6250 * jax.random.uniform(jax.random.fold_in(_gk, 3), (200000,)) ** 2.0).astype(jnp.int32), 99999)
        _o = jnp.argsort(dst, stable=True)
        src = src[_o]
        dst = dst[_o]
        edge_attr_16 = 0.000196303 + 1.00016 * jax.random.normal(jax.random.fold_in(_gk, 12), (200000, 16), jnp.float32)
        edge_attr_8 = -0.00010739 + 0.99994 * jax.random.normal(jax.random.fold_in(_gk, 13), (200000, 8), jnp.float32)
        edge_weight = jax.random.uniform(jax.random.fold_in(_gk, 15), (200000,), jnp.float32, 0.0, 1)
        return (x, src, dst, edge_attr_16, edge_attr_8, edge_weight)
    x, src, dst, edge_attr_16, edge_attr_8, edge_weight = _rec_inputs()

    def _L0_gnn_setup():
        import jax, jax.numpy as jnp
        import numpy as np
        N_NODES = 3125
        N_EDGES = 100000
        D = 64
        H = 8
        HD = D // H
        RAD_IN = 8
        SPH_IN = 16
        HIDDEN = 64
        AVG_NUM_NEIGHBORS = 32.0

        def _mlp2(x, W1, b1, W2, b2):
            return jax.nn.silu(x @ W1 + b1) @ W2 + b2
        key = jax.random.key(seed)
        ks = jax.random.split(key, 16)
        glorot = jax.nn.initializers.glorot_uniform()
        return {'node_feats': jax.random.normal(ks[0], (N_NODES, D), jnp.float32), 'edge_feats': jax.random.normal(ks[1], (N_EDGES, RAD_IN), jnp.float32), 'chi_scalar': jax.random.normal(ks[2], (N_EDGES, SPH_IN), jnp.float32), 'cutoffs': jax.random.uniform(ks[3], (N_EDGES,), jnp.float32), 'W_rad1': glorot(ks[4], (RAD_IN, HIDDEN), jnp.float32), 'b_rad1': jnp.zeros((HIDDEN,), jnp.float32), 'W_rad2': glorot(ks[5], (HIDDEN, H * HD), jnp.float32), 'b_rad2': jnp.zeros((H * HD,), jnp.float32), 'W_sph1': glorot(ks[6], (SPH_IN, HIDDEN), jnp.float32), 'b_sph1': jnp.zeros((HIDDEN,), jnp.float32), 'W_sph2': glorot(ks[7], (HIDDEN, H * HD), jnp.float32), 'b_sph2': jnp.zeros((H * HD,), jnp.float32), 'Wq': glorot(ks[8], (D, D), jnp.float32), 'Wk': glorot(ks[9], (D, D), jnp.float32), 'Wv': glorot(ks[10], (D, D), jnp.float32), 'senders': jax.random.randint(ks[11], (N_EDGES,), 0, N_NODES, jnp.int32), 'receivers': jax.random.randint(ks[12], (N_EDGES,), 0, N_NODES, jnp.int32)}
    _L0_gnn_all = _L0_gnn_setup()
    _L0_gnn_in = {k: v for k, v in _L0_gnn_all.items() if k in ('W_rad1', 'b_rad1', 'W_rad2', 'b_rad2', 'W_sph1', 'b_sph1', 'W_sph2', 'b_sph2', 'Wq', 'Wk', 'Wv')}
    del _L0_gnn_all

    def _L1_gnn_setup():
        import jax, jax.numpy as jnp
        import numpy as np
        N = 6250
        M = 78125
        D = 64
        K = 3
        LAMBDA_AMP = 0.1

        def _gcn_norm(edge_index, edge_weight, n):
            src, dst = (edge_index[0], edge_index[1])
            loop = jnp.arange(n, dtype=src.dtype)
            src = jnp.concatenate([src, loop])
            dst = jnp.concatenate([dst, loop])
            w = jnp.concatenate([edge_weight, jnp.ones((n,), edge_weight.dtype)])
            deg = jax.ops.segment_sum(w, dst, num_segments=n)
            dinv = jnp.where(deg > 0, jax.lax.rsqrt(jnp.maximum(deg, 1e-12)), 0.0)
            norm = dinv[src] * w * dinv[dst]
            return (src, dst, norm)

        def _spmm(x, src, dst, w, n):
            return jax.ops.segment_sum(w[:, None] * x[src], dst, num_segments=n)

        def _proximal_l21(x, lam):
            row_norm = jnp.sqrt(jnp.sum(x * x, axis=1))
            score = jnp.maximum(row_norm - lam, 0.0)
            scale = jnp.where(row_norm > 0, score / jnp.maximum(row_norm, 1e-12), 0.0)
            return scale[:, None] * x
        key = jax.random.key(seed)
        k1, k2, k3 = jax.random.split(key, 3)
        x = jax.random.normal(k1, (N, D), dtype=jnp.float32)
        edge_index = jax.random.randint(k2, (2, M), 0, N, dtype=jnp.int64)
        edge_weight = jax.random.uniform(k3, (M,), dtype=jnp.float32)
        return {'x': x, 'edge_index': edge_index, 'edge_weight': edge_weight}
    _L1_gnn_all = _L1_gnn_setup()
    _L1_gnn_in = {k: v for k, v in _L1_gnn_all.items() if k in ()}
    del _L1_gnn_all

    def _L2_gnn_setup():
        import jax, jax.numpy as jnp
        import numpy as np
        N_NODES = 6250
        N_EDGES = 100000
        N_CHANNELS = 64
        HIDDEN_DIM = 32
        POLY_DEGREE = 5
        DEG_CLAMP = 1000000.0
        key = jax.random.key(seed)
        k1, k2, k3, k4, k5, k6 = jax.random.split(key, 6)
        x = jax.random.normal(k1, (N_NODES, N_CHANNELS), dtype=jnp.float32)
        edge_index = jax.random.randint(k2, (2, N_EDGES), 0, N_NODES, dtype=jnp.int32)
        fan1 = N_CHANNELS + 4
        W1 = jax.random.uniform(k3, (HIDDEN_DIM, fan1), jnp.float32, -1.0, 1.0) / np.sqrt(fan1)
        b1 = jax.random.uniform(k4, (HIDDEN_DIM,), jnp.float32, -1.0, 1.0) / np.sqrt(fan1)
        W2 = jax.random.uniform(k5, (POLY_DEGREE + 1, HIDDEN_DIM), jnp.float32, -1.0, 1.0) / np.sqrt(HIDDEN_DIM)
        b2 = jax.random.uniform(k6, (POLY_DEGREE + 1,), jnp.float32, -1.0, 1.0) / np.sqrt(HIDDEN_DIM)
        return {'x': x, 'edge_index': edge_index, 'W1': W1, 'b1': b1, 'W2': W2, 'b2': b2}
    _L2_gnn_all = _L2_gnn_setup()
    _L2_gnn_in = {k: v for k, v in _L2_gnn_all.items() if k in ('W1', 'b1', 'W2', 'b2')}
    del _L2_gnn_all

    def _L3_gnn_setup():
        import jax, jax.numpy as jnp
        import numpy as np
        N_NODES = 6250
        N_EDGES = 50000
        D = 64

        def _gcn_conv(x, src, dst, W, b):
            N = x.shape[0]
            h = x @ W
            deg = 1.0 + jax.ops.segment_sum(jnp.ones_like(dst, dtype=h.dtype), dst, num_segments=N)
            dinv = jax.lax.rsqrt(deg)
            norm = dinv[src] * dinv[dst]
            msg = h[src] * norm[:, None]
            agg = jax.ops.segment_sum(msg, dst, num_segments=N)
            return agg + h * (1.0 / deg)[:, None] + b
        key = jax.random.key(seed)
        k1, k2, k3, k4 = jax.random.split(key, 4)
        x = jax.random.normal(k1, (N_NODES, D), dtype=jnp.float32)
        edge_index = jax.random.randint(k2, (2, N_EDGES), 0, N_NODES, dtype=jnp.int64)
        scale = 1.0 / np.sqrt(D)
        W1 = jax.random.normal(k3, (D, D), dtype=jnp.float32) * scale
        W2 = jax.random.normal(k4, (D, D), dtype=jnp.float32) * scale
        b1 = jnp.zeros((D,), dtype=jnp.float32)
        b2 = jnp.zeros((D,), dtype=jnp.float32)
        return {'x': x, 'edge_index': edge_index, 'W1': W1, 'b1': b1, 'W2': W2, 'b2': b2}
    _L3_gnn_all = _L3_gnn_setup()
    _L3_gnn_in = {k: v for k, v in _L3_gnn_all.items() if k in ('W1', 'b1', 'W2', 'b2')}
    del _L3_gnn_all
    return {'x': x, 'src': src, 'dst': dst, 'edge_attr_16': edge_attr_16, 'edge_attr_8': edge_attr_8, 'edge_weight': edge_weight, 'L0_gnn_W_rad1': _L0_gnn_in['W_rad1'], 'L0_gnn_b_rad1': _L0_gnn_in['b_rad1'], 'L0_gnn_W_rad2': _L0_gnn_in['W_rad2'], 'L0_gnn_b_rad2': _L0_gnn_in['b_rad2'], 'L0_gnn_W_sph1': _L0_gnn_in['W_sph1'], 'L0_gnn_b_sph1': _L0_gnn_in['b_sph1'], 'L0_gnn_W_sph2': _L0_gnn_in['W_sph2'], 'L0_gnn_b_sph2': _L0_gnn_in['b_sph2'], 'L0_gnn_Wq': _L0_gnn_in['Wq'], 'L0_gnn_Wk': _L0_gnn_in['Wk'], 'L0_gnn_Wv': _L0_gnn_in['Wv'], 'L2_gnn_W1': _L2_gnn_in['W1'], 'L2_gnn_b1': _L2_gnn_in['b1'], 'L2_gnn_W2': _L2_gnn_in['W2'], 'L2_gnn_b2': _L2_gnn_in['b2'], 'L3_gnn_W1': _L3_gnn_in['W1'], 'L3_gnn_b1': _L3_gnn_in['b1'], 'L3_gnn_W2': _L3_gnn_in['W2'], 'L3_gnn_b2': _L3_gnn_in['b2']}

def reference(x, src, dst, edge_attr_16, edge_attr_8, edge_weight, L0_gnn_W_rad1, L0_gnn_b_rad1, L0_gnn_W_rad2, L0_gnn_b_rad2, L0_gnn_W_sph1, L0_gnn_b_sph1, L0_gnn_W_sph2, L0_gnn_b_sph2, L0_gnn_Wq, L0_gnn_Wk, L0_gnn_Wv, L2_gnn_W1, L2_gnn_b1, L2_gnn_W2, L2_gnn_b2, L3_gnn_W1, L3_gnn_b1, L3_gnn_W2, L3_gnn_b2):
    import jax
    import jax.numpy as jnp

    def _L0_gnn_ref(node_feats, edge_feats, chi_scalar, cutoffs, W_rad1, b_rad1, W_rad2, b_rad2, W_sph1, b_sph1, W_sph2, b_sph2, Wq, Wk, Wv, senders, receivers):
        import jax, jax.numpy as jnp
        import numpy as np
        N_NODES = 3125
        N_EDGES = 100000
        D = 64
        H = 8
        HD = D // H
        RAD_IN = 8
        SPH_IN = 16
        HIDDEN = 64
        AVG_NUM_NEIGHBORS = 32.0

        def _mlp2(x, W1, b1, W2, b2):
            return jax.nn.silu(x @ W1 + b1) @ W2 + b2
        w_ij = _mlp2(edge_feats, W_rad1, b_rad1, W_rad2, b_rad2)
        w_ij = w_ij + _mlp2(chi_scalar, W_sph1, b_sph1, W_sph2, b_sph2)
        w_ij = w_ij.reshape(-1, H, HD)
        q_i = (node_feats @ Wq).reshape(-1, H, HD)[receivers]
        k_j = (node_feats @ Wk).reshape(-1, H, HD)[senders]
        alpha = (q_i * w_ij * k_j).sum(axis=-1) / jnp.sqrt(jnp.float32(HD))
        alpha = alpha * cutoffs[:, None]
        v_j = (node_feats @ Wv)[senders].reshape(-1, H, HD)
        out = jax.ops.segment_sum(alpha[..., None] * v_j, receivers, num_segments=node_feats.shape[0]) / AVG_NUM_NEIGHBORS
        return out.reshape(-1, H * HD)

    def _L1_gnn_ref(x, edge_index, edge_weight):
        import jax, jax.numpy as jnp
        import numpy as np
        N = 6250
        M = 78125
        D = 64
        K = 3
        LAMBDA_AMP = 0.1

        def _gcn_norm(edge_index, edge_weight, n):
            src, dst = (edge_index[0], edge_index[1])
            loop = jnp.arange(n, dtype=src.dtype)
            src = jnp.concatenate([src, loop])
            dst = jnp.concatenate([dst, loop])
            w = jnp.concatenate([edge_weight, jnp.ones((n,), edge_weight.dtype)])
            deg = jax.ops.segment_sum(w, dst, num_segments=n)
            dinv = jnp.where(deg > 0, jax.lax.rsqrt(jnp.maximum(deg, 1e-12)), 0.0)
            norm = dinv[src] * w * dinv[dst]
            return (src, dst, norm)

        def _spmm(x, src, dst, w, n):
            return jax.ops.segment_sum(w[:, None] * x[src], dst, num_segments=n)

        def _proximal_l21(x, lam):
            row_norm = jnp.sqrt(jnp.sum(x * x, axis=1))
            score = jnp.maximum(row_norm - lam, 0.0)
            scale = jnp.where(row_norm > 0, score / jnp.maximum(row_norm, 1e-12), 0.0)
            return scale[:, None] * x
        n = x.shape[0]
        src, dst, w = _gcn_norm(edge_index, edge_weight, n)
        gamma = 1.0 / (2.0 * (1.0 - LAMBDA_AMP))
        hh = x
        for _ in range(K):
            lx = x - _spmm(x, src, dst, w, n)
            y = x - gamma * 2.0 * (1.0 - LAMBDA_AMP) * lx
            x = hh + _proximal_l21(y - hh, gamma * LAMBDA_AMP)
        return x

    def _L2_gnn_ref(x, edge_index, W1, b1, W2, b2):
        import jax, jax.numpy as jnp
        import numpy as np
        N_NODES = 6250
        N_EDGES = 100000
        N_CHANNELS = 64
        HIDDEN_DIM = 32
        POLY_DEGREE = 5
        DEG_CLAMP = 1000000.0
        N, C = x.shape
        E = edge_index.shape[1]
        row, col = (edge_index[0], edge_index[1])
        deg = jax.ops.segment_sum(jnp.ones((E,), x.dtype), col, num_segments=N)
        deg_inv_sqrt = jnp.minimum(deg ** (-0.5), DEG_CLAMP)
        deg_inv_sqrt = jnp.where(jnp.isinf(deg_inv_sqrt), 0.0, deg_inv_sqrt)
        norm = deg_inv_sqrt[row] * deg_inv_sqrt[col]
        x_mean = x.mean(axis=0)
        stats = jnp.stack([x.mean(), x.std(ddof=1), jnp.asarray(N, x.dtype), jnp.asarray(E, x.dtype)])
        coeff_in = jnp.concatenate([x_mean, stats])
        h = jax.nn.relu(W1 @ coeff_in + b1)
        coeffs = jax.nn.softmax(W2 @ h + b2)
        result = coeffs[0] * x
        tx = x
        for k in range(1, POLY_DEGREE + 1):
            tx = jax.ops.segment_sum(norm[:, None] * tx[col], row, num_segments=N)
            result = result + coeffs[k] * tx
        return result

    def _L3_gnn_ref(x, edge_index, W1, b1, W2, b2):
        import jax, jax.numpy as jnp
        import numpy as np
        N_NODES = 6250
        N_EDGES = 50000
        D = 64

        def _gcn_conv(x, src, dst, W, b):
            N = x.shape[0]
            h = x @ W
            deg = 1.0 + jax.ops.segment_sum(jnp.ones_like(dst, dtype=h.dtype), dst, num_segments=N)
            dinv = jax.lax.rsqrt(deg)
            norm = dinv[src] * dinv[dst]
            msg = h[src] * norm[:, None]
            agg = jax.ops.segment_sum(msg, dst, num_segments=N)
            return agg + h * (1.0 / deg)[:, None] + b
        src, dst = (edge_index[0], edge_index[1])
        h = jax.nn.relu(_gcn_conv(x, src, dst, W1, b1))
        return _gcn_conv(h, src, dst, W2, b2)
    edge_index = jnp.stack([src, dst])
    x = _layernorm(x + _L0_gnn_ref(x, edge_attr_8, edge_attr_16, edge_weight, L0_gnn_W_rad1, L0_gnn_b_rad1, L0_gnn_W_rad2, L0_gnn_b_rad2, L0_gnn_W_sph1, L0_gnn_b_sph1, L0_gnn_W_sph2, L0_gnn_b_sph2, L0_gnn_Wq, L0_gnn_Wk, L0_gnn_Wv, src, dst), axis=-1)
    x = _layernorm(x + _L1_gnn_ref(x, edge_index, edge_weight), axis=-1)
    x = _layernorm(x + _L2_gnn_ref(x, edge_index, L2_gnn_W1, L2_gnn_b1, L2_gnn_W2, L2_gnn_b2), axis=-1)
    x = _layernorm(x + _L3_gnn_ref(x, edge_index, L3_gnn_W1, L3_gnn_b1, L3_gnn_W2, L3_gnn_b2), axis=-1)
    return x

_drawn_inputs = setup_inputs


def setup_inputs(seed=0):
    import zlib

    import numpy as np

    out = dict(_drawn_inputs(seed))
    spreads = {'L0_gnn_b_rad1': (0.0, 0.8),
     'L0_gnn_b_rad2': (0.0, 0.689),
     'L0_gnn_b_sph1': (0.0, 0.8),
     'L0_gnn_b_sph2': (0.0, 0.555),
     'L3_gnn_b1': (0.0, 0.1),
     'L3_gnn_b2': (0.0, 0.1)}
    factors = {}
    for name, (base, spread) in spreads.items():
        noise = np.random.default_rng([zlib.crc32(name.encode()), seed]).standard_normal(out[name].shape)
        drawn = base * np.exp(spread * noise) if base else spread * noise
        out[name] = jnp.asarray(drawn.astype(out[name].dtype))
    for name, factor in factors.items():
        out[name] = (out[name] * factor).astype(out[name].dtype)
    return out
```

```python
import concourse.bass as bass
from concourse import mybir
from contextlib import ExitStack, nullcontext
import numpy as np

F32, BF16, I32, I16 = mybir.dt.float32, mybir.dt.bfloat16, mybir.dt.int32, mybir.dt.int16
ALU, ACT, AX = mybir.AluOpType, mybir.ActivationFunctionType, mybir.AxisListType

N_NODES, D = 6250, 64
N_EDGES = 200000
NB = 50
NL = N_NODES // NB
TE = 125
NT = N_EDGES // TE
G = 8
NG = NT // G
CAP = 128
ROW = 72
DST_LANE, SRC_LANE, W1, ONE, DST, SRC = 64, 65, 66, 69, 70, 71
N_SLOTS = NB * CAP * NB
SPILL_ROWS = N_EDGES + 128
HID = 64


class Semaphores:
    made = {}

    def __init__(self, nc):
        self.nc, self.held = nc, []

    def __enter__(self):
        return self

    def __call__(self, name):
        if name not in self.made:
            self.made[name] = self.nc.alloc_semaphore(name=name)
        self.held.append(self.made[name])
        return self.made[name]

    def of_pool_dma(self, name):
        return self.nc.alloc_semaphore(name=name)

    def __exit__(self, *failure):
        with self.nc.Block() as blk:
            @blk.sync
            def _(sp):
                for held in self.held:
                    sp.sem_clear(held)


def prepare(nc, io, tbl, key_rows, block_rows, sorted_rows, zeros, zeroed):
    with ExitStack() as ctx:
        sb = lambda name, shape, dt: ctx.enter_context(nc.sbuf_tensor(f"prep_{name}", shape, dt))
        sem = ctx.enter_context(Semaphores(nc))
        ends = sb("ends", [NL, 2, NT], I32)
        node = sb("node", [NL, NT], F32)
        lane = sb("lane", [NL, NT], F32)
        block_d = sb("block_d", [NL, NT], F32)
        block_s = sb("block_s", [NL, NT], F32)
        weight = sb("weight", [NL, NT], F32)
        key16 = ends[:, 0, 0:NT // 2].bitcast(I16)
        block16 = sb("block16", [NL, NT], BF16)
        cols_in, rows_in, step = sem("cols_in"), sem("rows_in"), sem("step")
        cols_read, rows_ready, rows_out = sem("cols_read"), sem("rows_ready"), sem("rows_out")
        zeros_made = sem("zeros_made")
        with nc.Block() as blk:
            @blk.gpsimd
            def _(pool):
                pool.memset(zeros[:], 0.0).then_inc(zeros_made, 1)

            @blk.scalar
            def _(act):
                act.wait_ge(zeros_made, 1)
                view = sorted_rows[0:N_SLOTS, :].rearrange("(k b) c -> k (b c)", b=NB // 2)
                for b in range(2 * NB):
                    act.dma_start(view[b * CAP:(b + 1) * CAP, :], zeros[:]).then_inc(zeroed, 16)

            @blk.sync
            def _(sp):
                sp.dma_start(ends[:, 0, :], io["dst_cols"]).then_inc(cols_in, 16)
                sp.dma_start(ends[:, 1, :], io["src_cols"]).then_inc(cols_in, 16)
                sp.dma_start(weight[:], io["weight_cols"]).then_inc(cols_in, 16)
                sp.wait_ge(cols_read, 2)
                sp.dma_start(ends[:, 0, :], io["dst"].rearrange("(q c) -> q c", q=NL)).then_inc(rows_in, 16)
                sp.dma_start(ends[:, 1, :], io["src"].rearrange("(q c) -> q c", q=NL)).then_inc(rows_in, 16)
                sp.wait_ge(rows_ready, 1)
                sp.dma_start(key_rows.rearrange("(q c) -> q c", q=NL), key16).then_inc(rows_out, 16)
                sp.dma_start(block_rows.rearrange("(q c) -> q c", q=NL), block16[:]).then_inc(rows_out, 16)
                sp.wait_ge(rows_out, 32)

            @blk.vector
            def _(dve):
                n = [0]

                def link(ins):
                    n[0] += 1
                    ins.then_inc(step, 1)
                    dve.wait_ge(step, n[0])

                def split(which, block, read):
                    link(dve.tensor_copy(node[:], ends[:, which, :]))
                    if read:
                        dve.sem_inc(cols_read, 1)
                    link(dve.tensor_scalar(lane[:], node[:], 1.0 / NB, -0.49, ALU.mult, ALU.add))
                    link(dve.tensor_scalar(lane[:], lane[:], 12582912.0, None, ALU.add))
                    link(dve.tensor_scalar(lane[:], lane[:], 12582912.0, None, ALU.subtract))
                    link(dve.scalar_tensor_tensor(block[:], lane[:], -float(NB), node[:], ALU.mult, ALU.add))

                dve.wait_ge(cols_in, 48)
                split(0, block_d, True)
                link(dve.tensor_scalar(tbl[:, :, 0], lane[:], 1.0, None, ALU.add))
                link(dve.tensor_copy(tbl[:, :, 6], node[:]))
                split(1, block_s, True)
                link(dve.tensor_scalar(tbl[:, :, 1], lane[:], 1.0, None, ALU.add))
                link(dve.tensor_copy(tbl[:, :, 7], node[:]))
                rest = lane
                link(dve.tensor_copy(block16[:], weight[:]))
                link(dve.tensor_copy(tbl[:, :, 2], block16[:]))
                link(dve.tensor_tensor(rest[:], weight[:], block16[:], ALU.subtract))
                link(dve.tensor_copy(block16[:], rest[:]))
                link(dve.tensor_copy(tbl[:, :, 3], block16[:]))
                link(dve.tensor_tensor(tbl[:, :, 4], rest[:], block16[:], ALU.subtract))
                link(dve.tensor_scalar(tbl[:, :, 5], weight[:], 0.0, 1.0, ALU.mult, ALU.add))
                link(dve.tensor_copy(tbl[:, :, 8], weight[:]))
                link(dve.tensor_copy(tbl[:, :, 9], block_d[:]))
                link(dve.tensor_copy(tbl[:, :, 10], block_s[:]))
                dve.wait_ge(rows_in, 32)
                split(0, block_d, False)
                split(1, block_s, False)
                link(dve.tensor_copy(block16[:], block_d[:]))
                dve.scalar_tensor_tensor(key16, block_d[:], float(NB), block_s[:], ALU.mult, ALU.add)\
                   .then_inc(rows_ready, 1)


def sort_edges(nc, io, tbl, key_rows, block_rows, sorted_rows, zeros, zeroed, n_spilled):
    with ExitStack() as ctx:
        sb = lambda name, shape, dt: ctx.enter_context(nc.sbuf_tensor(f"sort_{name}", shape, dt))
        pb = lambda name, shape: ctx.enter_context(nc.psum_tensor(f"sort_{name}", shape, F32))
        sem = ctx.enter_context(Semaphores(nc))
        two = range(2)
        iota_blocks = sb("iota_blocks", [TE, NB], F32)
        tri = sb("tri", [TE, 2, TE], F32)
        before = sb("before", [TE, 2, TE], BF16)
        ones = sb("ones", [TE, TE], BF16)
        w1 = sb("w1", [24, 128], F32)
        b1 = sb("b1", [128, 1], F32)
        w2 = sb("w2", [128, D], F32)
        b2 = sb("b2", [TE, 3, D], F32)
        key_row = [sb(f"key_row{u}", [TE, G * TE], I16) for u in two]
        block_row = [sb(f"block_row{u}", [NB, G * TE], BF16) for u in two]
        attrs = [sb(f"attrs{u}", [24, G * TE], F32) for u in two]
        grp = [sb(f"grp{u}", [TE, G, 13], F32) for u in two]
        hot_d = [sb(f"hot_d{u}", [TE, G, NB], BF16) for u in two]
        hot_s = [sb(f"hot_s{u}", [TE, G, NB], BF16) for u in two]
        hot_dt = [sb(f"hot_dt{u}", [NB, G * TE], BF16) for u in two]
        hidden = [sb(f"hidden{u}", [128, G * TE], F32) for u in two]
        count = [sb(f"count{u}", [NB, NB], BF16) for u in two]
        same = sb("same", [TE, G, TE], BF16)
        picked = sb("picked", [TE, G, NB], F32)
        rank_in = sb("rank_in", [TE, G], F32)
        base = sb("base", [TE, G], F32)
        rank = sb("rank", [TE, G], F32)
        slot_row = sb("slot_row", [TE, G], F32)
        spills = sb("spills", [TE, G], BF16)
        spill_ps = sb("spill_ps", [TE, 2, G], F32)
        one_cols = sb("one_cols", [TE, G], F32)
        upto = sb("upto", [TE, G], F32)
        spill_row = sb("spill_row", [TE, G], F32)
        so_far = sb("so_far", [TE, 1], F32)
        biased = sb("biased", [TE, G, D], F32)
        rows = [sb(f"rows{u}", [TE, G, ROW], F32) for u in two]
        row_at = [sb(f"row_at{u}", [TE, G], I32) for u in two]
        pad_f = sb("pad_f", [TE, 1], F32)
        pad_at = sb("pad_at", [TE, 1], I32)
        lane_col = sb("lane_col", [TE, 1], F32)
        ps_h = [pb(f"ps_h{i}", [128, 512]) for i in two]
        ps_c = pb("ps_c", [128, 512])
        ps_r = [pb(f"ps_r{u}", [128, 512]) for u in two]
        ps_m = [pb(f"ps_m{u}", [128, 512]) for u in two]
        ps_f = pb("ps_f", [128, 512])

        const_in, made = sem("const_in"), sem("made")
        loaded = [sem(f"loaded{u}") for u in two]
        step, hots, rows_read, hidden_ps = sem("step"), sem("hots"), sem("rows_read"), sem("hidden_ps")
        silu, counted, snapped, based = sem("silu"), sem("counted"), sem("snapped"), sem("based")
        mixed, flagged, prefixed, rows_ready = sem("mixed"), sem("flagged"), sem("prefixed"), sem("rows_ready")
        stored = [sem.of_pool_dma(f"row_stored{u}") for u in two]
        padded, taken = sem.of_pool_dma("padded"), sem("taken")
        H = G // 2
        N_CONST = 16 * 12

        with nc.Block() as blk:
            @blk.sync
            def _(sp):
                for dst, src in ((iota_blocks[:], io["iota"][0:TE, 0:NB]), (lane_col[:], io["lanes"][0:TE, :]),
                                 (tri[:, 0, :], io["tri"][0:TE, 0:TE]), (tri[:, 1, :], io["tri_t"][0:TE, 0:TE]),
                                 (b1[0:HID, :], io["b_sph1"].rearrange("(p a) -> p a", a=1)),
                                 (b1[HID:128, :], io["b_rad1"].rearrange("(p a) -> p a", a=1)),
                                 (w2[0:HID, :], io["W_sph2"]), (w2[HID:128, :], io["W_rad2"]),
                                 (b2[:, 0, :], io["b_sph2"].rearrange("(a n) -> a n", a=1).to_broadcast([TE, D])),
                                 (b2[:, 1, :], io["b_rad2"].rearrange("(a n) -> a n", a=1).to_broadcast([TE, D]))):
                    sp.dma_start(dst, src).then_inc(const_in, 16)
                sp.wait_ge(made, 1)
                sp.dma_start(w1[0:16, 0:HID], io["W_sph1"]).then_inc(const_in, 16)
                sp.dma_start(w1[16:24, HID:128], io["W_rad1"]).then_inc(const_in, 16)

                def loads(u, edges):
                    sp.dma_start(key_row[u][:], key_rows[edges].rearrange("(a n) -> a n", a=1)
                                 .to_broadcast([TE, G * TE])).then_inc(loaded[u], 16)
                    sp.dma_start(block_row[u][:], block_rows[edges].rearrange("(a n) -> a n", a=1)
                                 .to_broadcast([NB, G * TE])).then_inc(loaded[u], 16)
                    sp.dma_start(attrs[u][0:16, :], io["attr16_t"][:, edges]).then_inc(loaded[u], 16)
                    sp.dma_start(attrs[u][16:24, :], io["attr8_t"][:, edges]).then_inc(loaded[u], 16)

                for u in two:
                    loads(u, slice(u * G * TE, (u + 1) * G * TE))
                with sp.Fori(0, NG // 2 - 1) as it:
                    for u in two:
                        sp.wait_ge(rows_read, 2 * it + (u + 1))
                        sp.sem_inc(taken, 1)
                        sp.wait_ge(hidden_ps, 4 * it + (2 * u + 2))
                        sp.sem_inc(taken, 1)
                        loads(u, bass.ds((2 * it + (2 + u)) * (G * TE), G * TE))

            @blk.gpsimd
            def _(pool):
                pool.memset(w1[:], 0.0).then_inc(made, 1)
                for u in two:
                    pool.memset(rows[u][:], 0.0)
                pool.memset(one_cols[:], 1.0)
                pool.memset(so_far[:], 0.0)
                pool.memset(count[0][:], 0.0)
                pool.memset(ones[:], 1.0).then_inc(made, 1)
                pool.wait_ge(zeroed, 32 * NB)

                with pool.Fori(0, NG // 2) as it:
                    for u in two:
                        pool.wait_ge(rows_ready, 2 * it + (u + 1))
                        pool.sem_inc(taken, 1)
                        for j in range(G):
                            pool.indirect_dma_start(
                                out=sorted_rows, out_offset=bass.IndirectOffsetOnAxis(row_at[u][:, j:j + 1], 0),
                                in_=rows[u][:, j, :], in_offset=None,
                                bounds_check=N_SLOTS + SPILL_ROWS - 1, oob_is_err=False).then_inc(stored[u], 16)
                pool.wait_ge(rows_ready, NG + 1)
                pool.indirect_dma_start(
                    out=sorted_rows, out_offset=bass.IndirectOffsetOnAxis(pad_at[:, 0:1], 0),
                    in_=zeros[0:TE, 0:ROW], in_offset=None,
                    bounds_check=N_SLOTS + SPILL_ROWS - 1, oob_is_err=False).then_inc(padded, 16)
                for u in two:
                    pool.wait_ge(stored[u], 16 * G * (NG // 2))
                pool.wait_ge(padded, 16)

            @blk.scalar
            def _(act):
                act.wait_ge(const_in, N_CONST)

                def group(n, first):
                    u = 1 if first == 1 else n[1]
                    n = n[0]
                    for j in range(G):
                        if j in (1, 3):
                            h = j // 2
                            act.wait_ge(hidden_ps, 2 * n + (h + 1))
                            if h == 0 and first is None:
                                act.wait_ge(mixed, n - 1)
                            act.activation(hidden[u][:, h * H * TE:(h + 1) * H * TE], ps_h[h][:, 0:H * TE],
                                           ACT.Silu, bias=b1[:, 0:1]).then_inc(silu, 1)
                        act.wait_ge(counted, n * G + (j + 1))
                        act.activation(count[(j + 1) % 2][:], ps_c[0:NB, 0:NB], ACT.Copy).then_inc(snapped, 1)

                group((0, 0), 0)
                group((1, 1), 1)
                with act.Fori(1, NG // 2) as it:
                    for u in two:
                        group((2 * it + u, u), None)

            @blk.tensor
            def _(pe):
                pe.wait_ge(made, 2)
                pe.wait_ge(const_in, N_CONST)
                nc.tensor.matmul(ps_c[0:NB, 0:NB], count[0][:], count[0][:], start=True, stop=True,
                                 skip_group_check=True)

                def group(n, it, u, first):
                    pe.wait_ge(loaded[u], 64 * it + 64)
                    for h in two:
                        if first != 0:
                            pe.wait_ge(silu, 2 * n + (h - 1))
                        nc.tensor.matmul(ps_h[h][:, 0:H * TE], w1[:], attrs[u][:, h * H * TE:(h + 1) * H * TE],
                                         start=True, stop=True).then_inc(hidden_ps, 1)
                    pe.wait_ge(hots, n + 1)
                    for j in range(G):
                        if not (first == 0 and j == 0):
                            pe.wait_ge(snapped, n * G + j)
                        last = nc.tensor.matmul(ps_r[u][0:TE, j * NB:(j + 1) * NB], hot_dt[u][:, j * TE:(j + 1) * TE],
                                                count[j % 2][:], start=True, stop=True, skip_group_check=True)
                        if j == G - 1:
                            last.then_inc(based, 1)
                        nc.tensor.matmul(ps_c[0:NB, 0:NB], hot_d[u][:, j, :], hot_s[u][:, j, :], start=False,
                                         stop=True, skip_group_check=True).then_inc(counted, 1)
                        if j == H - 1 and first != 0:
                            prefixes(n)
                        if j == H:
                            pe.wait_ge(silu, 2 * n + 2)
                        if j >= H:
                            for t in (2 * (j - H), 2 * (j - H) + 1):
                                last = nc.tensor.matmul(ps_m[u][0:TE, t * D:(t + 1) * D],
                                                        hidden[u][:, t * TE:(t + 1) * TE], w2[:], start=True,
                                                        stop=True, skip_group_check=True)
                    last.then_inc(mixed, 1)

                def prefixes(n):
                    pe.wait_ge(flagged, n)
                    nc.tensor.matmul(ps_f[0:TE, 0:G], before[:, 1, :], spills[:], start=True, stop=True,
                                     skip_group_check=True)
                    nc.tensor.matmul(ps_f[0:TE, G:2 * G], ones[:], spills[:], start=True, stop=True,
                                     skip_group_check=True).then_inc(prefixed, 1)

                group(0, 0, 0, 0)
                group(1, 0, 1, 1)
                with pe.Fori(1, NG // 2) as it:
                    for u in two:
                        group(2 * it + u, it, u, None)
                prefixes(NG)

            @blk.vector
            def _(dve):
                dve.wait_ge(const_in, N_CONST)
                dve.wait_ge(made, 2)
                dve.tensor_tensor(b2[:, 2, :], b2[:, 0, :], b2[:, 1, :], ALU.add)
                dve.tensor_copy(before[:], tri[:])

                def group_hots(g, it, u, first):
                    g_is_0 = isinstance(g, int) and g == 0
                    dve.wait_ge(loaded[u], 64 * it + 64)
                    if not first:
                        dve.wait_ge(mixed, g - 1)
                    dve.tensor_copy(grp[u][:, :, 0:11], tbl[:, bass.ds(g * G, G), :]).then_inc(step, 1)
                    dve.wait_ge(step, 1 if g_is_0 else STEPS * g - (STEPS - 2))
                    dve.scalar_tensor_tensor(grp[u][:, :, 11], grp[u][:, :, 9], float(NB), grp[u][:, :, 10],
                                             ALU.mult, ALU.add)
                    dve.scalar_tensor_tensor(grp[u][:, :, 12], grp[u][:, :, 9], float(NB * CAP), grp[u][:, :, 10],
                                             ALU.mult, ALU.add)
                    iota3 = iota_blocks[:].unsqueeze(1).to_broadcast([TE, G, NB])
                    dve.tensor_tensor(hot_d[u][:], iota3, grp[u][:, :, 9:10].to_broadcast([TE, G, NB]), ALU.is_equal)
                    dve.tensor_tensor(hot_s[u][:], iota3, grp[u][:, :, 10:11].to_broadcast([TE, G, NB]), ALU.is_equal)
                    dve.tensor_scalar(hot_dt[u][:], block_row[u][:], lane_col[0:NB, 0:1], None,
                                      ALU.is_equal).then_inc(hots, 1)

                def link(ins, value):
                    ins.then_inc(step, 1)
                    dve.wait_ge(step, value)

                STEPS = 12

                def places(g, it, u, done):
                    at = STEPS * g + 2 if done else STEPS * g + 1
                    k = [0]

                    def nxt(ins):
                        k[0] += 1
                        link(ins, at + k[0])
                    for j in range(G):
                        last = dve.scalar_tensor_tensor(same[:, j, :], key_row[u][:, j * TE:(j + 1) * TE],
                                                        grp[u][:, j, 11:12], before[:, 0, :], ALU.is_equal, ALU.mult,
                                                        accum_out=rank_in[:, j:j + 1])
                    last.then_inc(rows_read, 1)
                    dve.wait_ge(rows_read, g + 1)
                    dve.wait_ge(based, g + 1)
                    nxt(dve.tensor_tensor(picked[:], ps_r[u][0:TE, 0:G * NB].rearrange("p (g b) -> p g b", g=G),
                                          hot_s[u][:], ALU.mult))
                    nxt(dve.tensor_reduce(base[:], picked[:], AX.X, ALU.add))
                    nxt(dve.tensor_tensor(rank[:], rank_in[:], base[:], ALU.add))
                    dve.tensor_scalar(spills[:], rank[:], float(CAP), None, ALU.is_ge).then_inc(flagged, 1)
                    nxt(dve.scalar_tensor_tensor(slot_row[:], rank[:], float(NB), grp[u][:, :, 12], ALU.mult, ALU.add))
                    dve.wait_ge(mixed, g + 1)
                    dve.wait_ge(stored[u], 16 * G * it)
                    nxt(dve.tensor_tensor(biased[:], ps_m[u][0:TE, :].rearrange("p (g d) -> p g d", g=G),
                                          b2[:, 2:3, :].to_broadcast([TE, G, D]), ALU.add))
                    dve.tensor_tensor(rows[u][:, :, 0:D], biased[:], grp[u][:, :, 8:9].to_broadcast([TE, G, D]), ALU.mult)
                    dve.tensor_copy(rows[u][:, :, D:ROW], grp[u][:, :, 0:8])
                    dve.wait_ge(prefixed, g + 1)
                    nxt(dve.tensor_copy(spill_ps[:], ps_f[0:TE, 0:2 * G].rearrange("p (a g) -> p a g", a=2)))
                    nxt(dve.tensor_tensor_scan(upto[:], one_cols[:], spill_ps[:, 1, :], so_far[:, 0:1],
                                               ALU.mult, ALU.add))
                    dve.tensor_copy(so_far[:], upto[:, G - 1:G])
                    nxt(dve.tensor_tensor(spill_row[:], spill_ps[:, 0, :], spill_ps[:, 1, :], ALU.subtract))
                    nxt(dve.tensor_tensor(spill_row[:], spill_row[:], upto[:], ALU.add))
                    nxt(dve.scalar_tensor_tensor(spill_row[:], spill_row[:], float(N_SLOTS), slot_row[:],
                                                 ALU.add, ALU.subtract))
                    nxt(dve.tensor_tensor(spill_row[:], spill_row[:], spills[:], ALU.mult))
                    dve.tensor_tensor(row_at[u][:], spill_row[:], slot_row[:], ALU.add).then_inc(rows_ready, 1)
                    assert k[0] == STEPS - 1

                group_hots(0, 0, 0, True)
                group_hots(1, 0, 1, True)
                places(0, 0, 0, 1)
                with dve.Fori(1, NG // 2) as it:
                    group_hots(2 * it, it, 0, False)
                    places(2 * it - 1, it - 1, 1, 1)
                    group_hots(2 * it + 1, it, 1, False)
                    places(2 * it, it, 0, 1)
                places(NG - 1, NG // 2 - 1, 1, 0)
                at = STEPS * NG
                link(dve.tensor_scalar(pad_f[:], lane_col[:], so_far[:, 0:1], float(N_SLOTS), ALU.add, ALU.add), at + 1)
                dve.tensor_copy(pad_at[:], pad_f[:]).then_inc(rows_ready, 1)
                dve.wait_ge(rows_ready, NG + 1)
                link(dve.tensor_scalar(pad_f[:], so_far[:], 1.0 / TE, -0.496, ALU.mult, ALU.add), at + 2)
                link(dve.tensor_scalar(pad_f[:], pad_f[:], 12582912.0, None, ALU.add), at + 3)
                link(dve.tensor_scalar(pad_f[:], pad_f[:], 12582911.0, None, ALU.subtract), at + 4)
                dve.tensor_copy(n_spilled[:], pad_f[:])



def project(nc, tag, x, weights, out, ident, n_out):
    with ExitStack() as ctx:
        sb = lambda name, shape, dt: ctx.enter_context(nc.sbuf_tensor(f"{tag}_{name}", shape, dt))
        pb = lambda name, shape: ctx.enter_context(nc.psum_tensor(f"{tag}_{name}", shape, F32))
        sem = ctx.enter_context(Semaphores(nc))
        two = range(2)
        block = [sb(f"block{u}", [NL, D], F32) for u in two]
        block_t = [sb(f"block_t{u}", [D, NL], F32) for u in two]
        ps_t = [pb(f"ps_t{u}", [128, 512]) for u in two]
        ps_o = [pb(f"ps_o{u}", [128, 512]) for u in two]
        taken = sem("taken")
        staged, turned, turned_sb, product, kept = (sem(n) for n in ("staged", "turned", "turned_sb", "product", "kept"))
        with nc.Block() as blk:
            @blk.scalar
            def _(act):
                act.sem_inc(turned, 2)
                act.sem_inc(product, 2)
                with act.Fori(0, NB // 2) as it:
                    for u in two:
                        act.wait_ge(turned, 2 * it + (u + 1))
                        act.activation(block[u][:], x[:, bass.ds(2 * it + u, 1), :].rearrange("p a d -> p (a d)"),
                                       ACT.Copy).then_inc(staged, 1)
                    for u in two:
                        act.wait_ge(turned, 2 * it + (u + 3))
                        act.wait_ge(product, 2 * it + (u + 1))
                        act.activation(block_t[u][:], ps_t[u][0:D, 0:NL], ACT.Copy).then_inc(turned_sb, 1)

            @blk.tensor
            def _(pe):
                pe.sem_inc(kept, 2)
                with pe.Fori(0, NB // 2) as it:
                    for u in two:
                        pe.wait_ge(staged, 2 * it + (u + 1))
                        pe.sem_inc(taken, 1)
                        nc.tensor.transpose(ps_t[u][0:D, 0:NL], block[u][:], ident[0:NL, 0:NL]).then_inc(turned, 1)
                    for u in two:
                        pe.wait_ge(turned_sb, 2 * it + (u + 1))
                        pe.wait_ge(kept, 2 * it + (u + 1))
                        nc.tensor.matmul(ps_o[u][0:NL, 0:n_out], block_t[u][:], weights, start=True,
                                         stop=True).then_inc(product, 1)

            @blk.vector
            def _(dve):
                with dve.Fori(0, NB // 2) as it:
                    for u in two:
                        dve.wait_ge(product, 2 * it + (u + 3))
                        dve.tensor_copy(out[:, bass.ds(2 * it + u, 1), :].rearrange("p a d -> p (a d)"),
                                        ps_o[u][0:NL, 0:n_out]).then_inc(kept, 1)


def load_tables(nc, io, x, w_qkv, ident, iota1, ident16):
    with ExitStack() as ctx:
        loaded = ctx.enter_context(Semaphores(nc))("tables_loaded")
        iota_f = ctx.enter_context(nc.sbuf_tensor("iota_f", [128, 128], F32))
        with nc.Block() as blk:
            @blk.sync
            def _(sp):
                sp.dma_start(x[:], io["x"].rearrange("(p b) d -> p b d", b=NB)).then_inc(loaded, 16)
                for i, name in enumerate(("Wq", "Wk", "Wv")):
                    sp.dma_start(w_qkv[:, i * D:(i + 1) * D], io[name]).then_inc(loaded, 16)
                sp.dma_start(ident[:], io["ident"]).then_inc(loaded, 16)
                sp.dma_start(iota_f[:], io["iota"]).then_inc(loaded, 16)
                sp.wait_ge(loaded, 96)

            @blk.vector
            def _(dve):
                dve.wait_ge(loaded, 96)
                dve.tensor_scalar(iota1[:], iota_f[:], 1.0, None, ALU.add)
                dve.tensor_copy(ident16[:], ident[:])


def split_qkv(nc, qkv, q_parts, kv_parts, qkv_rows):
    with ExitStack() as ctx:
        sem = ctx.enter_context(Semaphores(nc))
        step, out = sem("step"), sem("qkv_out")
        with nc.Block() as blk:
            @blk.sync
            def _(sp):
                sp.dma_start(qkv_rows.rearrange("(p b) d -> p (b d)", b=NB), qkv[:].rearrange("p b d -> p (b d)"))\
                  .then_inc(out, 16)
                sp.wait_ge(out, 16)

            @blk.vector
            def _(dve):
                n = [0]

                def link(ins):
                    n[0] += 1
                    ins.then_inc(step, 1)
                    dve.wait_ge(step, n[0])

                def split(parts, whole):
                    for i in range(2):
                        link(dve.tensor_copy(parts[:, :, i, :], whole))
                        link(dve.tensor_tensor(whole, whole, parts[:, :, i, :], ALU.subtract))
                    dve.tensor_copy(parts[:, :, 2, :], whole)

                dve.wait_ge(out, 16)
                split(q_parts, qkv[:, :, 0:D])
                split(kv_parts, qkv[:, :, D:3 * D])


NP = 10
HP = NP // 2
N_HG, N_RP = NB // NP, NB // 2
MW = 3 * D + 4


def build_graph(nc, io, sorted_rows, q_parts, kv_parts, iota1, ident16, acc, weighted, counts, counts_t):
    with ExitStack() as ctx:
        sb = lambda name, shape, dt: ctx.enter_context(nc.sbuf_tensor(f"graph_{name}", shape, dt))
        pb = lambda name, shape, dt=F32: ctx.enter_context(nc.psum_tensor(f"graph_{name}", shape, dt))
        sem = ctx.enter_context(Semaphores(nc))
        two, five = range(2), range(5)
        edges = [sb(f"edges{h}", [128, 2, HP, ROW], F32) for h in two]
        kv = sb("kv", [NL, NP, 3, 2 * D], BF16)
        q = sb("q", [NL, 2, 3, D], BF16)
        hot = [sb(f"hot{b}", [128, 2, 2, 128], BF16) for b in five]
        heavy = [sb(f"heavy{b}", [128, 2, 3, 128], BF16) for b in five]
        hot_t = [sb(f"hot_t{u}", [128, 2, 2, 128], BF16) for u in two]
        qw = sb("qw", [128, 2, D], F32)
        qwk = sb("qwk", [128, 2, D], F32)
        alpha = sb("alpha", [128, 16], F32)
        msg = [sb(f"msg{u}", [128, 2, D], F32) for u in two]
        rest = [sb(f"rest{i}", [128, 2, D], F32) for i in two]
        parts = [sb(f"parts{b}", [128, 2, MW], BF16) for b in five]
        st_w = [sb(f"st_w{h}", [128, 2, HP, NL], F32) for h in two]
        st_c = [sb(f"st_c{h}", [128, 2, HP, 128], BF16) for h in two]
        st_t = [sb(f"st_t{h}", [128, HP, 2, 128], BF16) for h in two]
        none = sb("none", [128, 2 * MW], BF16)
        ps_t = [pb(f"ps_t{u}", [128, 2, 2, 256], BF16) for u in two]
        ps_w = pb("ps_w", [128, 4, 128])
        ps_c = [pb(f"ps_c{u}", [128, 2, 2, 128]) for u in two]
        ps_l = [pb(f"ps_l{u}", [128, 512]) for u in two]
        ps_o = pb("ps_o", [128, 512])

        loaded = [sem(f"loaded{h}") for h in two]
        stored = [sem(f"stored{h}") for h in two]
        cleared, kv_ready, q_ready, hots = sem("cleared"), sem("kv_ready"), sem("q_ready"), sem("hots")
        turned, turned_sb, blocks, blocks_sb = sem("turned"), sem("turned_sb"), sem("blocks"), sem("blocks_sb")
        weights_sb = sem("weights_sb")
        looked, msgs, split = sem("looked"), sem("msgs"), sem("split")
        summed, added, step, pstep, taken = sem("summed"), sem("sums_added"), sem("step"), sem("pstep"), sem("taken")
        B_SUMMED, B_BLOCKS_SB, B_LOOKED, B_MSGS, B_SPLIT = 5, 2, 2, 2, 5
        by_slot = sorted_rows[0:N_SLOTS, :].rearrange("(h r s) c -> h r s c", r=CAP, s=NB)

        with nc.Block() as blk:
            @blk.sync
            def _(sp):
                with sp.Fori(0, N_HG) as hg:
                    with sp.Fori(0, N_RP) as rp:
                        for h in two:
                            sp.wait_ge(split, (hg * N_RP + rp) * NP + (HP * h))
                            sp.sem_inc(taken, 1)
                            sp.dma_start(edges[h][:].rearrange("r h s c -> r h (s c)"),
                                         by_slot[bass.ds(2 * rp, 2), :, bass.ds(hg * NP + HP * h, HP), :]
                                         .rearrange("h r s c -> r h (s c)")).then_inc(loaded[h], 16)

            @blk.gpsimd
            def _(pool):
                pool.sem_inc(split, B_SPLIT)
                pool.memset(acc[:], 0.0)
                pool.memset(none[:], 0.0).then_inc(cleared, 1)
                with pool.Fori(0, N_HG) as hg:
                    with pool.Fori(0, N_RP) as rp:
                        n = hg * N_RP + rp
                        for s in range(NP):
                            u, b, h, k = s % 2, s % 5, s // HP, s % HP
                            pool.wait_ge(msgs, n * NP + (s + 1 + B_MSGS))
                            pool.wait_ge(summed, n * NP + (s + 1))
                            if s in (0, HP):
                                pool.wait_ge(loaded[h], 16 * n + 16)
                            pool.sem_inc(taken, 1)
                            pool.tensor_copy(parts[b][:, :, 0:D], msg[u][:]).then_inc(pstep, 1)
                            pool.wait_ge(pstep, (n * NP + s) * 3 + 1)
                            pool.tensor_tensor(rest[0][:], msg[u][:], parts[b][:, :, 0:D], ALU.subtract).then_inc(pstep, 1)
                            pool.tensor_copy(parts[b][:, :, 3 * D:MW], edges[h][:, :, k, W1:W1 + 4])
                            pool.wait_ge(pstep, (n * NP + s) * 3 + 2)
                            pool.sem_inc(taken, 1)
                            pool.tensor_copy(parts[b][:, :, D:2 * D], rest[0][:]).then_inc(pstep, 1)
                            pool.wait_ge(pstep, (n * NP + s) * 3 + 3)
                            pool.tensor_tensor(parts[b][:, :, 2 * D:3 * D], rest[0][:], parts[b][:, :, D:2 * D],
                                               ALU.subtract).then_inc(split, 1)
                            pool.wait_ge(split, n * NP + (s + 1 + B_SPLIT))

            @blk.scalar
            def _(act):
                act.sem_inc(blocks_sb, B_BLOCKS_SB)
                with act.Fori(0, N_HG) as hg:
                    with act.Fori(0, N_RP) as rp:
                        n = hg * N_RP + rp
                        for s in range(NP):
                            u, h, k = s % 2, s // HP, s % HP
                            act.wait_ge(turned, n * NP + (s + 1))
                            act.wait_ge(looked, n * NP + (s + 1))
                            act.activation(hot_t[u][:], ps_t[u][:, :, :, 0:128], ACT.Copy).then_inc(turned_sb, 1)
                            act.wait_ge(blocks, n * NP + (s + 1))
                            if k == 0:
                                act.wait_ge(stored[h], 48 * n)
                            act.activation(st_w[h][:, :, k, :], ps_w[:, 0:2, 0:NL], ACT.Copy).then_inc(weights_sb, 1)
                            act.activation(st_c[h][:, :, k, :], ps_c[u][:, 0], ACT.Copy)
                            act.activation(st_t[h][:, k, :, :], ps_c[u][:, 1], ACT.Copy).then_inc(blocks_sb, 1)
                            if k == HP - 1:
                                act.wait_ge(blocks_sb, n * NP + (s + 1 + B_BLOCKS_SB))
                                s0, d0 = hg * NP + HP * h, 2 * rp
                                act.dma_start(weighted[bass.ds(d0, 2), :, bass.ds(s0, HP), :]
                                              .rearrange("h p s d -> p h (s d)"),
                                              st_w[h][:].rearrange("p h s d -> p h (s d)")).then_inc(stored[h], 16)
                                act.dma_start(counts[bass.ds(d0, 2), :, bass.ds(s0, HP), :]
                                              .rearrange("h p s d -> p h (s d)"),
                                              st_c[h][:].rearrange("p h s d -> p h (s d)")).then_inc(stored[h], 16)
                                act.dma_start(counts_t[bass.ds(s0, HP), :, bass.ds(d0, 2), :]
                                              .rearrange("s p h d -> p s (h d)"),
                                              st_t[h][:].rearrange("p s h d -> p s (h d)")).then_inc(stored[h], 16)
                for h in two:
                    act.wait_ge(stored[h], 48 * N_HG * N_RP)

            @blk.tensor
            def _(pe):
                pe.sem_inc(summed, B_SUMMED)
                pe.sem_inc(looked, B_LOOKED)
                pe.wait_ge(cleared, 1)
                with pe.Fori(0, N_HG) as hg:
                    with pe.Fori(0, N_RP) as rp:
                        n = hg * N_RP + rp
                        pe.wait_ge(added, n)
                        nc.tensor.matmul(ps_o[:, 0:2 * MW], none[:, 0:128], none[:], start=True, stop=True,
                                         skip_group_check=True)
                        for s in range(NP + 3):
                            if s < NP:
                                u, b = s % 2, s % 5
                                pe.wait_ge(hots, n * NP + (s + 1))
                                for t in two:
                                    for w in two:
                                        last = nc.tensor.transpose(ps_t[u][:, t, w, 0:128], hot[b][:, t, w], ident16[:])
                                last.then_inc(turned, 1)
                                pe.wait_ge(blocks_sb, n * NP + (s + 1))
                                for t in two:
                                    dst, src = hot[b][:, t, 0], hot[b][:, t, 1]
                                    nc.tensor.matmul(ps_c[u][:, 1, t], dst, src, start=True, stop=True,
                                                     skip_group_check=True)
                                    nc.tensor.matmul(ps_c[u][:, 0, t], src, dst, start=True, stop=True,
                                                     skip_group_check=True)
                                pe.wait_ge(weights_sb, n * NP + s)
                                for t in two:
                                    for i in range(3):
                                        last = nc.tensor.matmul(ps_w[:, t], hot[b][:, t, 1], heavy[b][:, t, i],
                                                                start=i == 0, stop=i == 2, skip_group_check=True)
                                last.then_inc(blocks, 1)
                            if 1 <= s <= NP:
                                r = s - 1
                                u = r % 2
                                if r == 0:
                                    pe.wait_ge(kv_ready, hg + 1)
                                    pe.wait_ge(q_ready, n + 1)
                                pe.wait_ge(turned_sb, n * NP + (r + 1))
                                pe.wait_ge(msgs, n * NP + (r + 1))
                                for t in two:
                                    for i in range(3):
                                        nc.tensor.matmul(ps_l[u][:, t * 2 * D:(t + 1) * 2 * D], hot_t[u][0:NL, t, 1],
                                                         kv[:, r, i], start=i == 0, stop=i == 2, skip_group_check=True)
                                    for i in range(3):
                                        last = nc.tensor.matmul(ps_l[u][:, (4 + t) * D:(5 + t) * D],
                                                                hot_t[u][0:NL, t, 0], q[:, t, i], start=i == 0,
                                                                stop=i == 2, skip_group_check=True)
                                last.then_inc(looked, 1)
                            if s >= 3:
                                r = s - 3
                                b = r % 5
                                pe.wait_ge(split, n * NP + (r + 1 + B_SPLIT))
                                for t in two:
                                    last = nc.tensor.matmul(ps_o[:, t * MW:(t + 1) * MW], hot[b][:, t, 0], parts[b][:, t],
                                                            start=False, stop=True, skip_group_check=True)
                                last.then_inc(summed, 1)

            @blk.vector
            def _(dve):
                dve.sem_inc(msgs, B_MSGS)
                dve.wait_ge(cleared, 1)
                with dve.Fori(0, N_HG) as hg:
                    dve.tensor_copy(kv[:].rearrange("p s i d -> p (s i d)"),
                                    kv_parts[:, bass.ds(hg * NP, NP)].rearrange("p s i d -> p (s i d)")).then_inc(kv_ready, 1)
                    with dve.Fori(0, N_RP) as rp:
                        n = hg * N_RP + rp
                        dve.tensor_copy(q[:].rearrange("p t i d -> p (t i d)"),
                                        q_parts[:, bass.ds(2 * rp, 2)].rearrange("p t i d -> p (t i d)")).then_inc(q_ready, 1)

                        def one_hots(s):
                            b, h, k = s % 5, s // HP, s % HP
                            if k == 0:
                                dve.wait_ge(loaded[h], 16 * n + 16)
                            dve.wait_ge(summed, n * NP + (s + 1))
                            for t in two:
                                dst = edges[h][:, t, k, DST_LANE:DST_LANE + 1]
                                for i in range(3):
                                    dve.tensor_scalar(heavy[b][:, t, i], iota1[:], dst,
                                                      edges[h][:, t, k, W1 + i:W1 + i + 1], ALU.is_equal, ALU.mult)
                                dve.tensor_scalar(hot[b][:, t, 0], iota1[:], dst, None, ALU.is_equal)
                                last = dve.tensor_scalar(hot[b][:, t, 1], iota1[:],
                                                         edges[h][:, t, k, SRC_LANE:SRC_LANE + 1], None, ALU.is_equal)
                            last.then_inc(hots, 1)

                        def messages(s):
                            u, h, k = s % 2, s // HP, s % HP
                            i = (n * NP + s) * 3
                            dve.wait_ge(looked, n * NP + (s + 1 + B_LOOKED))
                            q_e = ps_l[u][:, 4 * D:6 * D].rearrange("p (t d) -> p t d", t=2)
                            kv_e = ps_l[u][:, 0:4 * D].rearrange("p (t a d) -> p t a d", t=2, a=2)
                            dve.tensor_tensor(qw[:], q_e, edges[h][:, :, k, 0:D], ALU.mult).then_inc(step, 1)
                            dve.wait_ge(step, i + 1)
                            dve.tensor_tensor(qwk[:], kv_e[:, :, 0], qw[:], ALU.mult).then_inc(step, 1)
                            dve.wait_ge(step, i + 2)
                            dve.wait_ge(msgs, n * NP + (s + B_MSGS))
                            dve.tensor_reduce(alpha[:], qwk[:].rearrange("p t (a c) -> p (t a) c", c=8), AX.X, ALU.add)\
                               .then_inc(step, 1)
                            dve.wait_ge(step, i + 3)
                            dve.wait_ge(split, n * NP + (s - 1 + B_SPLIT))
                            dve.tensor_tensor(msg[u][:].rearrange("p t (a c) -> p t a c", c=8),
                                              kv_e[:, :, 1].rearrange("p t (a c) -> p t a c", c=8),
                                              alpha[:].rearrange("p (t a) -> p t a", t=2).unsqueeze(3)
                                              .to_broadcast([128, 2, 8, 8]), ALU.mult).then_inc(msgs, 1)

                        for s in range(NP):
                            one_hots(s)
                            if s >= 2:
                                messages(s - 2)
                        messages(NP - 2)
                        messages(NP - 1)
                        dve.wait_ge(summed, n * NP + (NP + B_SUMMED))
                        dve.wait_ge(added, n)
                        at = acc[:, bass.ds(2 * rp, 2), :].rearrange("p h c -> p (h c)")
                        dve.tensor_tensor(at, at, ps_o[0:NL, 0:2 * MW], ALU.add).then_inc(added, 1)


YB = NB + 1


def spill_messages(nc, io, sorted_rows, qkv_rows, y_rows, y_sb, n_spilled, ident):
    W = D + 2
    with ExitStack() as ctx:
        sb = lambda name, shape, dt: ctx.enter_context(nc.sbuf_tensor(f"spill_{name}", shape, dt))
        pb = lambda name, shape, dt=F32: ctx.enter_context(nc.psum_tensor(f"spill_{name}", shape, dt))
        sem = ctx.enter_context(Semaphores(nc))
        edges = sb("edges", [TE, ROW], F32)
        before = sb("before", [TE, TE], F32)
        lane_col = sb("lane_col", [TE, 1], F32)
        zeros = sb("zeros", [TE, YB * W], F32)
        dst_at, src_at, to = sb("dst_at", [TE, 1], I32), sb("src_at", [TE, 1], I32), sb("to", [TE, 1], I32)
        of_dst, of_src = sb("of_dst", [TE, 3 * D], F32), sb("of_src", [TE, 3 * D], F32)
        same, earlier = sb("same", [TE, TE], F32), sb("earlier", [TE, TE], F32)
        seen, spare = sb("seen", [TE, 1], F32), sb("spare", [TE, 1], F32)
        qw, alpha = sb("qw", [TE, D], F32), sb("alpha", [TE, 8], F32)
        msg = sb("msg", [TE, W], F32)
        total = sb("total", [TE, W], F32)
        ps_id, ps_sum = pb("ps_id", [128, 512]), pb("ps_sum", [128, 512])
        const, cleared, loaded, ids = (sem(n) for n in ("const", "cleared", "loaded", "ids"))
        row_ids, matched, summed, ready = (sem(n) for n in ("row_ids", "matched", "summed", "ready"))
        rows, added = sem.of_pool_dma("spill_rows"), sem.of_pool_dma("spill_added")
        step, taken, y_in = sem("step"), sem("taken"), sem("y_in")
        with nc.Block() as blk:
            @blk.sync
            def _(sp):
                n = sp.value_load(n_spilled[0:1, 0:1], min_val=1, max_val=NT + 1)
                sp.dma_start(before[:], io["tri"][0:TE, 0:TE]).then_inc(const, 16)
                sp.dma_start(lane_col[:], io["lanes"][0:TE, :]).then_inc(const, 16)
                sp.wait_ge(cleared, 1)
                sp.dma_start(y_rows.rearrange("(p b) c -> p (b c)", b=YB), zeros[:]).then_inc(const, 16)
                with sp.Fori(0, n) as t:
                    sp.wait_ge(added, 16 * t)
                    sp.sem_inc(taken, 1)
                    sp.dma_start(edges[:], sorted_rows[bass.ds(N_SLOTS + t * TE, TE), :]).then_inc(loaded, 16)
                sp.wait_ge(added, 16 * n)
                sp.sem_inc(taken, 1)
                sp.dma_start(y_sb, y_rows[0:N_NODES, :].rearrange("(p b) c -> p (b c)", b=NB)).then_inc(y_in, 16)
                sp.wait_ge(y_in, 16)

            @blk.gpsimd
            def _(pool):
                n = pool.value_load(n_spilled[0:1, 0:1], min_val=1, max_val=NT + 1)
                pool.memset(zeros[:], 0.0).then_inc(cleared, 1)
                pool.wait_ge(const, 48)
                with pool.Fori(0, n) as t:
                    pool.wait_ge(ids, t + 1)
                    pool.sem_inc(taken, 1)
                    pool.indirect_dma_start(out=of_dst[:], out_offset=None, in_=qkv_rows,
                                            in_offset=bass.IndirectOffsetOnAxis(dst_at[:, 0:1], 0)).then_inc(rows, 16)
                    pool.indirect_dma_start(out=of_src[:], out_offset=None, in_=qkv_rows,
                                            in_offset=bass.IndirectOffsetOnAxis(src_at[:, 0:1], 0)).then_inc(rows, 16)
                    pool.wait_ge(ready, t + 1)
                    pool.sem_inc(taken, 1)
                    pool.indirect_dma_start(out=y_rows, out_offset=bass.IndirectOffsetOnAxis(to[:, 0:1], 0),
                                            in_=total[:], in_offset=None, compute_op=ALU.add).then_inc(added, 16)
                    pool.wait_ge(added, 16 * t + 16)

            @blk.tensor
            def _(pe):
                n = pe.value_load(n_spilled[0:1, 0:1], min_val=1, max_val=NT + 1)
                with pe.Fori(0, n) as t:
                    pe.wait_ge(loaded, 16 * t + 16)
                    nc.tensor.matmul(ps_id[0:TE, 0:TE], edges[:, DST:DST + 1].to_broadcast([TE, TE]),
                                     ident[0:TE, 0:TE], start=True, stop=True).then_inc(row_ids, 1)
                    pe.wait_ge(matched, t + 1)
                    nc.tensor.matmul(ps_sum[0:TE, 0:W], same[:], msg[:], start=True, stop=True).then_inc(summed, 1)

            @blk.vector
            def _(dve):
                n = dve.value_load(n_spilled[0:1, 0:1], min_val=1, max_val=NT + 1)
                dve.wait_ge(const, 48)
                with dve.Fori(0, n) as t:
                    k = [0]

                    def link(ins):
                        k[0] += 1
                        ins.then_inc(step, 1)
                        dve.wait_ge(step, t * 9 + k[0])

                    dve.wait_ge(loaded, 16 * t + 16)
                    dve.tensor_copy(dst_at[:], edges[:, DST:DST + 1])
                    dve.tensor_copy(src_at[:], edges[:, SRC:SRC + 1]).then_inc(ids, 1)
                    dve.wait_ge(row_ids, t + 1)
                    link(dve.tensor_scalar(same[:], ps_id[0:TE, 0:TE], edges[:, DST:DST + 1], None, ALU.is_equal))
                    link(dve.tensor_tensor(earlier[:], same[:], before[:], ALU.mult))
                    link(dve.tensor_reduce(seen[:], earlier[:], AX.X, ALU.max))
                    link(dve.scalar_tensor_tensor(spare[:], lane_col[:], float(N_NODES), edges[:, DST:DST + 1],
                                                  ALU.add, ALU.subtract))
                    link(dve.tensor_tensor(spare[:], spare[:], seen[:], ALU.mult))
                    dve.tensor_tensor(to[:], spare[:], edges[:, DST:DST + 1], ALU.add)
                    dve.wait_ge(rows, 32 * t + 32)
                    link(dve.tensor_tensor(qw[:], of_dst[:, 0:D], edges[:, 0:D], ALU.mult))
                    link(dve.tensor_tensor(qw[:], qw[:], of_src[:, D:2 * D], ALU.mult))
                    link(dve.tensor_reduce(alpha[:], qw[:].rearrange("p (a c) -> p a c", c=8), AX.X, ALU.add))
                    dve.tensor_tensor(msg[:, 0:D].rearrange("p (a c) -> p a c", c=8),
                                      of_src[:, 2 * D:3 * D].rearrange("p (a c) -> p a c", c=8),
                                      alpha[:].unsqueeze(2).to_broadcast([TE, 8, 8]), ALU.mult)
                    dve.tensor_copy(msg[:, D + 1:W], edges[:, ONE:ONE + 1])
                    link(dve.tensor_reduce(msg[:, D:D + 1], edges[:, W1:W1 + 3], AX.X, ALU.add))
                    dve.sem_inc(matched, 1)
                    dve.wait_ge(summed, t + 1)
                    dve.tensor_copy(total[:], ps_sum[0:TE, 0:W]).then_inc(ready, 1)
                    dve.wait_ge(ready, t + 1)
                    assert k[0] == 9


def collect(nc, acc, y_sb, node_sums):
    W = D + 2
    y3 = y_sb.rearrange("p (b c) -> p b c", c=W)
    with ExitStack() as ctx:
        step = ctx.enter_context(Semaphores(nc))("step")
        with nc.Block() as blk:
            @blk.vector
            def _(dve):
                n = [0]

                def link(ins):
                    n[0] += 1
                    ins.then_inc(step, 1)
                    dve.wait_ge(step, n[0])
                for i in range(3):
                    link(dve.tensor_tensor(y3[:, :, 0:D], y3[:, :, 0:D], acc[:, :, i * D:(i + 1) * D], ALU.add))
                    link(dve.tensor_tensor(y3[:, :, D:D + 1], y3[:, :, D:D + 1], acc[:, :, 3 * D + i:3 * D + i + 1],
                                           ALU.add))
                link(dve.tensor_tensor(y3[:, :, D + 1:W], y3[:, :, D + 1:W], acc[:, :, MW - 1:MW], ALU.add))
                dve.tensor_copy(node_sums[:], y3)


def scale_of_degree(nc, tag, degree, extra, dinv):
    with ExitStack() as ctx:
        step = ctx.enter_context(Semaphores(nc))("step")
        with nc.Block() as blk:
            @blk.vector
            def _(dve):
                dve.tensor_scalar(dinv[:], degree, extra, 1e-12, ALU.add, ALU.max).then_inc(step, 1)
                dve.wait_ge(step, 2)
                dve.reciprocal(dinv[:], dinv[:])

            @blk.scalar
            def _(act):
                act.wait_ge(step, 1)
                act.activation(dinv[:], dinv[:], ACT.Sqrt).then_inc(step, 1)


def layer_norm(nc, tag, x, add, scale, tmp, out=None, out_rows=None):
    with ExitStack() as ctx:
        sb = lambda name, shape, dt: ctx.enter_context(nc.sbuf_tensor(f"{tag}_{name}", shape, dt))
        step = ctx.enter_context(Semaphores(nc))("step")
        rooted = ctx.enter_context(Semaphores(nc))("rooted")
        stored = ctx.enter_context(Semaphores(nc))("ln_stored")
        mean, var = sb("mean", [NL, NB], F32), sb("var", [NL, NB], F32)
        wide = lambda a: a[:].unsqueeze(2).to_broadcast([NL, NB, D])
        with nc.Block() as blk:
            @blk.vector
            def _(dve):
                n = [0]

                def link(ins):
                    n[0] += 1
                    ins.then_inc(step, 1)
                    dve.wait_ge(step, n[0])
                link(dve.scalar_tensor_tensor(x[:], add, scale, x[:], ALU.mult, ALU.add))
                link(dve.tensor_reduce(mean[:], x[:], AX.X, ALU.add))
                link(dve.tensor_scalar(mean[:], mean[:], 1.0 / D, None, ALU.mult))
                link(dve.tensor_tensor(x[:], x[:], wide(mean), ALU.subtract))
                link(dve.tensor_tensor(tmp[:], x[:], x[:], ALU.mult))
                link(dve.tensor_reduce(var[:], tmp[:], AX.X, ALU.add))
                link(dve.tensor_scalar(var[:], var[:], 1.0 / D, 1e-5, ALU.mult, ALU.add))
                dve.wait_ge(rooted, 1)
                link(dve.reciprocal(var[:], var[:]))
                link(dve.tensor_tensor(x[:], x[:], wide(var), ALU.mult))

            @blk.scalar
            def _(act):
                act.wait_ge(step, 7)
                act.activation(var[:], var[:], ACT.Sqrt).then_inc(rooted, 1)

            if out_rows is not None:
                @blk.sync
                def _(sp):
                    sp.wait_ge(step, 9)
                    sp.dma_start(out_rows.rearrange("(p b) d -> p b d", b=NB), x[:]).then_inc(stored, 16)
                    sp.wait_ge(stored, 16)


def spread(nc, tag, n_passes, matrix, exact, use_weight, gather, scatter, io, sorted_rows, rows, y_rows, n_spilled,
           ident, xs, parts, sums, y_sb, post_vector, post_scalar, before_vector=None):
    MC = matrix.shape[3]
    HR = NB // 2
    N2 = 24
    with ExitStack() as ctx:
        sb = lambda name, shape, dt: ctx.enter_context(nc.sbuf_tensor(f"{tag}_{name}", shape, dt))
        pb = lambda name, shape, dt=F32: ctx.enter_context(nc.psum_tensor(f"{tag}_{name}", shape, dt))
        sem = ctx.enter_context(Semaphores(nc))
        two = range(2)
        mat = [[sb(f"mat{u}{h}", [128, HR, MC], matrix.dtype) for h in two] for u in two]
        ps = [pb(f"ps{u}", [128, 512]) for u in two]
        edges = sb("edges", [TE, ROW], F32)
        before = sb("before", [TE, TE], F32)
        lane_col = sb("lane_col", [TE, 1], F32)
        zeros = sb("zeros", [TE, YB * D], F32)
        from_at, to = sb("from_at", [TE, 1], I32), sb("to", [TE, 1], I32)
        of_node = sb("of_node", [TE, D], F32)
        same, earlier = sb("same", [TE, TE], F32), sb("earlier", [TE, TE], F32)
        seen, spare, factor = sb("seen", [TE, 1], F32), sb("spare", [TE, 1], F32), sb("factor", [TE, 1], F32)
        msg, total = sb("msg", [TE, D], F32), sb("total", [TE, D], F32)
        ps_id, ps_sum = pb("ps_id", [128, 512]), pb("ps_sum", [128, 512])
        loaded = [[sem(f"mat_loaded{u}{h}") for h in two] for u in two]
        const, cleared, xs_ready, table = sem("const"), sem("cleared"), sem("xs_ready"), sem("table")
        got, ids, fetched, row_ids, matched = sem("got"), sem("ids"), sem.of_pool_dma(f"{tag}_fetched"), sem("row_ids"), sem("matched")
        summed, ready, added, y_in = sem("summed"), sem("ready"), sem.of_pool_dma(f"{tag}_added"), sem("y_in")
        row_done, row_kept, step, taken = sem("row_done"), sem("row_kept"), sem("step"), sem("taken")
        post = {n: sem(n) for n in ("post_v", "post_s")}

        passes = lambda e: e.Fori(0, n_passes) if n_passes > 1 else nullcontext(0)
        count = lambda e: e.value_load(n_spilled[0:1, 0:1], min_val=1, max_val=NT + 1)
        with nc.Block() as blk:
            @blk.sync
            def _(sp):
                n = count(sp)
                sp.dma_start(before[:], io["tri"][0:TE, 0:TE]).then_inc(const, 16)
                sp.dma_start(lane_col[:], io["lanes"][0:TE, :]).then_inc(const, 16)
                sp.wait_ge(cleared, 1)
                with passes(sp) as k:
                    sp.wait_ge(xs_ready, k + 1)
                    sp.sem_inc(taken, 1)
                    sp.dma_start(rows.rearrange("(p b) d -> p (b d)", b=NB),
                                 xs[:].rearrange("p b d -> p (b d)")).then_inc(table, 16)
                    sp.dma_start(y_rows.rearrange("(p b) c -> p (b c)", b=YB), zeros[:]).then_inc(table, 16)
                    with sp.Fori(0, n) as t:
                        sp.wait_ge(added, (k * n + t) * 16)
                        sp.sem_inc(taken, 1)
                        sp.dma_start(edges[:], sorted_rows[bass.ds(N_SLOTS + t * TE, TE), :]).then_inc(got, 16)
                    sp.wait_ge(added, (k * n + n) * 16)
                    sp.sem_inc(taken, 1)
                    sp.dma_start(y_sb[:].rearrange("p b d -> p (b d)"),
                                 y_rows[0:N_NODES, :].rearrange("(p b) c -> p (b c)", b=NB)).then_inc(y_in, 16)
                sp.wait_ge(y_in, 16 * n_passes)

            @blk.gpsimd
            def _(pool):
                n = count(pool)
                pool.memset(zeros[:], 0.0).then_inc(cleared, 1)
                with passes(pool) as k:
                    pool.wait_ge(table, 32 * k + 32)
                    pool.sem_inc(taken, 1)
                    with pool.Fori(0, n) as t:
                        pool.wait_ge(ids, k * n + t + 1)
                        pool.sem_inc(taken, 1)
                        pool.indirect_dma_start(out=of_node[:], out_offset=None, in_=rows,
                                                in_offset=bass.IndirectOffsetOnAxis(from_at[:, 0:1], 0))\
                            .then_inc(fetched, 16)
                        pool.wait_ge(ready, k * n + t + 1)
                        pool.sem_inc(taken, 1)
                        pool.indirect_dma_start(out=y_rows, out_offset=bass.IndirectOffsetOnAxis(to[:, 0:1], 0),
                                                in_=total[:], in_offset=None, compute_op=ALU.add).then_inc(added, 16)
                        pool.wait_ge(added, (k * n + t) * 16 + 16)

            @blk.scalar
            def _(act):
                def load(r, u):
                    for h in two:
                        src = matrix[bass.ds(r, 1), :, h * HR:(h + 1) * HR, :] if not isinstance(r, int) else \
                            matrix[r:r + 1, :, h * HR:(h + 1) * HR, :]
                        act.dma_start(mat[u][h][:].rearrange("p s d -> p (s d)"),
                                      src.rearrange("a p s d -> (a p) (s d)")).then_inc(loaded[u][h], 16)
                for u in two:
                    load(u, u)
                with passes(act) as k:
                    with act.Fori(0, N2) as r2:
                        for u in two:
                            act.wait_ge(row_done, k * NB + 2 * r2 + (u + 1))
                            load(2 * r2 + (2 + u), u)
                    for u in two:
                        act.wait_ge(row_done, k * NB + (2 * N2 + u + 1))
                        load(u, u)
                    post_scalar(act, k, post)
                for u in two:
                    for h in two:
                        act.wait_ge(loaded[u][h], 16 * (NB // 2 * n_passes + 1))

            @blk.tensor
            def _(pe):
                n = count(pe)
                with passes(pe) as k:
                    def dst_rows(r2):
                        for u in two:
                            r = 2 * r2 + u
                            if not (isinstance(r2, int) and False):
                                pe.wait_ge(row_kept, k * NB + r)
                            for h in two:
                                pe.wait_ge(loaded[u][h], (k * (NB // 2) + r2) * 16 + 16)
                                for s in range(HR):
                                    b = h * HR + s
                                    if exact:
                                        last = nc.tensor.matmul(ps[u][0:NL, 0:D], mat[u][h][0:NL, s, :], xs[:, b, :],
                                                                start=b == 0, stop=b == NB - 1)
                                    else:
                                        last = nc.tensor.matmul(ps[u][:, 0:3 * D], mat[u][h][0:NL, s, :],
                                                                parts[:, b].rearrange("p i d -> p (i d)"),
                                                                start=b == 0, stop=b == NB - 1)
                            last.then_inc(row_done, 1)

                    pe.wait_ge(xs_ready, k + 1)
                    pe.sem_inc(taken, 1)
                    with pe.Fori(0, N2 // 2) as r2:
                        dst_rows(r2)
                    with pe.Fori(0, n) as t:
                        pe.wait_ge(got, (k * n + t) * 16 + 16)
                        nc.tensor.matmul(ps_id[0:TE, 0:TE], edges[:, scatter:scatter + 1].to_broadcast([TE, TE]),
                                         ident[0:TE, 0:TE], start=True, stop=True).then_inc(row_ids, 1)
                        pe.wait_ge(matched, k * n + t + 1)
                        nc.tensor.matmul(ps_sum[0:TE, 0:D], same[:], msg[:], start=True, stop=True).then_inc(summed, 1)
                    with pe.Fori(N2 // 2, N2 + 1) as r2:
                        dst_rows(r2)

            @blk.vector
            def _(dve):
                n = count(dve)
                dve.wait_ge(const, 32)
                if before_vector is not None:
                    before_vector(dve)
                dve.sem_inc(xs_ready, 1)
                dve.sem_inc(row_kept, 1)
                with passes(dve) as k:
                    def keep_rows(r2):
                        for u in two:
                            r = 2 * r2 + u
                            dve.wait_ge(row_done, k * NB + (2 * r2 + (u + 1)))
                            to_row = sums[:, bass.ds(r, 1), :].rearrange("p a d -> p (a d)")
                            if exact:
                                dve.tensor_copy(to_row, ps[u][0:NL, 0:D]).then_inc(row_kept, 1)
                            else:
                                dve.tensor_reduce(to_row, ps[u][0:NL, 0:3 * D].rearrange("p (i d) -> p d i", i=3),
                                                  AX.X, ALU.add).then_inc(row_kept, 1)

                    with dve.Fori(0, N2 // 2) as r2:
                        keep_rows(r2)
                    with dve.Fori(0, n) as t:
                        m = k * n + t
                        i = [0]

                        def link(ins):
                            i[0] += 1
                            ins.then_inc(step, 1)
                            dve.wait_ge(step, m * 7 + i[0])
                        dve.wait_ge(got, m * 16 + 16)
                        dve.tensor_copy(from_at[:], edges[:, gather:gather + 1]).then_inc(ids, 1)
                        if use_weight:
                            link(dve.tensor_reduce(factor[:], edges[:, W1:W1 + 3], AX.X, ALU.add))
                        else:
                            link(dve.tensor_copy(factor[:], edges[:, ONE:ONE + 1]))
                        id_col = edges[:, scatter:scatter + 1]
                        dve.wait_ge(row_ids, m + 1)
                        link(dve.tensor_scalar(same[:], ps_id[0:TE, 0:TE], id_col, None, ALU.is_equal))
                        link(dve.tensor_tensor(earlier[:], same[:], before[:], ALU.mult))
                        link(dve.tensor_reduce(seen[:], earlier[:], AX.X, ALU.max))
                        link(dve.scalar_tensor_tensor(spare[:], lane_col[:], float(N_NODES), id_col, ALU.add,
                                                      ALU.subtract))
                        link(dve.tensor_tensor(spare[:], spare[:], seen[:], ALU.mult))
                        dve.tensor_tensor(to[:], spare[:], id_col, ALU.add)
                        dve.wait_ge(fetched, m * 16 + 16)
                        link(dve.tensor_scalar(msg[:], of_node[:], factor[:, 0:1], None, ALU.mult))
                        dve.sem_inc(matched, 1)
                        dve.wait_ge(summed, m + 1)
                        dve.tensor_copy(total[:], ps_sum[0:TE, 0:D]).then_inc(ready, 1)
                        dve.wait_ge(ready, m + 1)
                        assert i[0] == 7
                    with dve.Fori(N2 // 2, N2 + 1) as r2:
                        keep_rows(r2)
                    dve.wait_ge(row_kept, k * NB + (NB + 1))
                    dve.wait_ge(y_in, 16 * k + 16)
                    post_vector(dve, k, post)
                    dve.sem_inc(xs_ready, 1)


class Chain:

    def __init__(self, eng, sem, k, size):
        self.eng, self.sem, self.k, self.size, self.n = eng, sem, k, size, 0

    def __call__(self, ins):
        self.n += 1
        ins.then_inc(self.sem, 1)
        self.eng.wait_ge(self.sem, self.k * self.size + self.n if self.size else self.n)


def to_parts(link, dve, parts, whole, rest):
    link(dve.tensor_copy(parts[:, :, 0, :], whole[:]))
    link(dve.tensor_tensor(rest[:], whole[:], parts[:, :, 0, :], ALU.subtract))
    link(dve.tensor_copy(parts[:, :, 1, :], rest[:]))
    link(dve.tensor_tensor(parts[:, :, 2, :], rest[:], parts[:, :, 1, :], ALU.subtract))


def wide(col):
    return col[:].unsqueeze(2).to_broadcast([NL, NB, D])


def smooth(nc, shared, x, hh, dinv, xs, sums, y_sb, z, weighted):
    LAM = 0.1
    GAMMA = 1.0 / (2.0 * (1.0 - LAM))
    with ExitStack() as ctx:
        norm = ctx.enter_context(nc.sbuf_tensor("prox_norm", [NL, NB], F32))
        shrink = ctx.enter_context(nc.sbuf_tensor("prox_shrink", [NL, NB], F32))
        first = ctx.enter_context(Semaphores(nc))("first")

        def before_vector(dve):
            dve.tensor_copy(hh[:], x[:])
            dve.tensor_tensor(xs[:], x[:], wide(dinv), ALU.mult).then_inc(first, 1)
            dve.wait_ge(first, 1)

        def post_vector(dve, k, post):
            link = Chain(dve, post["post_v"], k, 15)
            link(dve.tensor_tensor(sums[:], sums[:], y_sb[:], ALU.add))
            link(dve.tensor_tensor(sums[:], sums[:], xs[:], ALU.add))
            link(dve.tensor_tensor(sums[:], sums[:], wide(dinv), ALU.mult))
            link(dve.tensor_tensor(sums[:], x[:], sums[:], ALU.subtract))
            link(dve.scalar_tensor_tensor(z[:], sums[:], -GAMMA * 2.0 * (1.0 - LAM), x[:], ALU.mult, ALU.add))
            link(dve.tensor_tensor(z[:], z[:], hh[:], ALU.subtract))
            link(dve.tensor_tensor(sums[:], z[:], z[:], ALU.mult))
            link(dve.tensor_reduce(norm[:], sums[:], AX.X, ALU.add))
            dve.wait_ge(post["post_s"], k + 1)
            link(dve.tensor_scalar(shrink[:], norm[:], GAMMA * LAM, 0.0, ALU.subtract, ALU.max))
            link(dve.tensor_scalar(norm[:], norm[:], 1e-12, None, ALU.max))
            link(dve.reciprocal(norm[:], norm[:]))
            link(dve.tensor_tensor(shrink[:], shrink[:], norm[:], ALU.mult))
            link(dve.tensor_tensor(z[:], z[:], wide(shrink), ALU.mult))
            link(dve.tensor_tensor(x[:], hh[:], z[:], ALU.add))
            link(dve.tensor_tensor(xs[:], x[:], wide(dinv), ALU.mult))

        def post_scalar(act, k, post):
            act.wait_ge(post["post_v"], k * 15 + 8)
            act.activation(norm[:], norm[:], ACT.Sqrt).then_inc(post["post_s"], 1)

        spread(nc, "smooth", 3, weighted, True, True, SRC, DST, *shared, xs, None, sums, y_sb, post_vector, post_scalar,
               before_vector)


def coefficients(nc, io, x, tmp, coeff):
    P, HD2 = 6, 32
    M = N_NODES * D
    with ExitStack() as ctx:
        sb = lambda name, shape, dt=F32: ctx.enter_context(nc.sbuf_tensor(f"coeff_{name}", shape, dt))
        pb = lambda name, shape: ctx.enter_context(nc.psum_tensor(f"coeff_{name}", shape, F32))
        sem = ctx.enter_context(Semaphores(nc))
        w1, w1t, w2t = sb("w1", [HD2, D + 4]), sb("w1t", [D, HD2]), sb("w2t", [HD2, P])
        b1, b2, ones = sb("b1", [HD2, 1]), sb("b2", [NL, P]), sb("ones", [NL, NL])
        by_feature, whole, mean, sq = sb("by_feature", [NL, D]), sb("whole", [NL, 1]), sb("mean", [NL, 1]), sb("sq", [NL, 1])
        feature_mean, stats, prod = sb("feature_mean", [D, 1]), sb("stats", [HD2, 4]), sb("prod", [HD2, 4])
        h, top, e, total = sb("h", [HD2, 1]), sb("top", [NL, 1]), sb("e", [NL, P]), sb("total", [NL, 1])
        ps_f, ps_m, ps_v, ps_h = (pb(n, [128, 512]) for n in ("ps_f", "ps_m", "ps_v", "ps_h"))
        ps_c = pb("ps_c", [128, 512])
        loaded, step, product, acted, cleared = (sem(n) for n in ("loaded", "step", "product", "acted", "cleared"))
        with nc.Block() as blk:
            @blk.sync
            def _(sp):
                for dst, src in ((w1, io["L2_gnn_W1"]), (w1t, io["L2_gnn_W1_t"][0:D, :]), (w2t, io["L2_gnn_W2_t"]),
                                 (b1, io["L2_gnn_b1"].rearrange("(p a) -> p a", a=1)),
                                 (b2, io["L2_gnn_b2"].rearrange("(a n) -> a n", a=1).to_broadcast([NL, P]))):
                    sp.dma_start(dst[:], src).then_inc(loaded, 16)

            @blk.gpsimd
            def _(pool):
                pool.memset(ones[:], 1.0).then_inc(cleared, 1)

            @blk.tensor
            def _(pe):
                pe.wait_ge(loaded, 80)
                pe.wait_ge(cleared, 1)
                pe.wait_ge(step, 2)
                nc.tensor.matmul(ps_f[0:D, 0:1], by_feature[:], ones[:, 0:1], start=True, stop=True)
                nc.tensor.matmul(ps_m[0:NL, 0:1], ones[:], whole[:], start=True, stop=True).then_inc(product, 1)
                pe.wait_ge(step, 6)
                nc.tensor.matmul(ps_v[0:NL, 0:1], ones[:], sq[:], start=True, stop=True).then_inc(product, 1)
                pe.wait_ge(step, 7)
                nc.tensor.matmul(ps_h[0:HD2, 0:1], w1t[:], feature_mean[:], start=True, stop=True).then_inc(product, 1)
                pe.wait_ge(step, 14)
                nc.tensor.matmul(ps_c[0:NL, 0:P], h[:].to_broadcast([HD2, NL]), w2t[:], start=True, stop=True)\
                  .then_inc(product, 1)

            @blk.scalar
            def _(act):
                act.wait_ge(step, 10)
                act.activation(stats[:, 1:2], stats[:, 1:2], ACT.Sqrt).then_inc(acted, 1)
                act.wait_ge(step, 17)
                act.activation(e[:], e[:], ACT.Exp).then_inc(acted, 1)

            @blk.vector
            def _(dve):
                link = Chain(dve, step, 0, 0)
                link(dve.tensor_reduce(by_feature[:], x[:].rearrange("p b d -> p d b"), AX.X, ALU.add))
                link(dve.tensor_reduce(whole[:], by_feature[:], AX.X, ALU.add))
                dve.wait_ge(product, 1)
                link(dve.tensor_scalar(mean[:], ps_m[0:NL, 0:1], 1.0 / M, None, ALU.mult))
                link(dve.tensor_scalar(tmp[:], x[:], mean[:, 0:1], None, ALU.subtract))
                link(dve.tensor_tensor(tmp[:], tmp[:], tmp[:], ALU.mult))
                link(dve.tensor_reduce(sq[:], tmp[:], AX.XY, ALU.add))
                link(dve.tensor_scalar(feature_mean[:], ps_f[0:D, 0:1], 1.0 / N_NODES, None, ALU.mult))
                dve.wait_ge(loaded, 80)
                link(dve.memset(stats[:, 3:4], float(N_EDGES)))
                link(dve.tensor_copy(stats[:, 0:1], mean[0:HD2, :]))
                dve.wait_ge(product, 2)
                link(dve.tensor_scalar(stats[:, 1:2], ps_v[0:HD2, 0:1], 1.0 / (M - 1), None, ALU.mult))
                link(dve.memset(stats[:, 2:3], float(N_NODES)))
                dve.wait_ge(acted, 1)
                link(dve.tensor_tensor(prod[:], stats[:], w1[:, D:D + 4], ALU.mult))
                dve.wait_ge(product, 3)
                link(dve.tensor_reduce(h[:], prod[:], AX.X, ALU.add))
                dve.scalar_tensor_tensor(h[:], ps_h[0:HD2, 0:1], b1[:, 0:1], h[:], ALU.add, ALU.add).then_inc(cleared, 1)
                dve.wait_ge(cleared, 2)
                link(dve.tensor_scalar(h[:], h[:], 0.0, None, ALU.max))
                dve.wait_ge(product, 4)
                link(dve.tensor_tensor(e[:], ps_c[0:NL, 0:P], b2[:], ALU.add))
                link(dve.tensor_reduce(top[:], e[:], AX.X, ALU.max))
                link(dve.tensor_scalar(e[:], e[:], top[:, 0:1], None, ALU.subtract))
                dve.wait_ge(acted, 2)
                link(dve.tensor_reduce(total[:], e[:], AX.X, ALU.add))
                link(dve.reciprocal(total[:], total[:]))
                link(dve.tensor_scalar(coeff[:], e[:], total[:, 0:1], None, ALU.mult))


def polynomial(nc, shared, x, result, dis, coeff, xs, parts, sums, y_sb, rest, counts_t):
    with ExitStack() as ctx:
        first = ctx.enter_context(Semaphores(nc))("first")
        now = ctx.enter_context(nc.sbuf_tensor("coeff_now", [NL, 1], F32))

        def before_vector(dve):
            link = Chain(dve, first, 0, 0)
            link(dve.tensor_scalar(result[:], x[:], coeff[:, 0:1], None, ALU.mult))
            link(dve.tensor_tensor(xs[:], x[:], wide(dis), ALU.mult))
            to_parts(link, dve, parts, xs, rest)

        def post_vector(dve, k, post):
            link = Chain(dve, post["post_v"], k, 9)
            link(dve.tensor_tensor(sums[:], sums[:], y_sb[:], ALU.add))
            link(dve.tensor_tensor(sums[:], sums[:], wide(dis), ALU.mult))
            link(dve.tensor_copy(now[:], coeff[:, bass.ds(k + 1, 1)]))
            link(dve.scalar_tensor_tensor(result[:], sums[:], now[:, 0:1], result[:], ALU.mult, ALU.add))
            link(dve.tensor_tensor(xs[:], sums[:], wide(dis), ALU.mult))
            to_parts(link, dve, parts, xs, rest)

        spread(nc, "poly", 5, counts_t, False, False, DST, SRC, *shared, xs, parts, sums, y_sb, post_vector,
               lambda act, k, post: None, before_vector)


def convolve(nc, tag, shared, h, bias, relu, dinv, xs, parts, sums, y_sb, rest, counts):
    with ExitStack() as ctx:
        first = ctx.enter_context(Semaphores(nc))("first")

        def before_vector(dve):
            link = Chain(dve, first, 0, 0)
            link(dve.tensor_tensor(xs[:], h[:], wide(dinv), ALU.mult))
            to_parts(link, dve, parts, xs, rest)

        def post_vector(dve, k, post):
            link = Chain(dve, post["post_v"], k, 5)
            link(dve.tensor_tensor(sums[:], sums[:], y_sb[:], ALU.add))
            link(dve.tensor_tensor(sums[:], sums[:], xs[:], ALU.add))
            link(dve.tensor_tensor(sums[:], sums[:], wide(dinv), ALU.mult))
            link(dve.tensor_tensor(h[:], sums[:], bias[:].unsqueeze(1).to_broadcast([NL, NB, D]), ALU.add))
            if relu:
                link(dve.tensor_scalar(h[:], h[:], 0.0, None, ALU.max))
            else:
                link(dve.tensor_copy(sums[:], h[:]))

        spread(nc, tag, 1, counts, False, False, SRC, DST, *shared, xs, parts, sums, y_sb, post_vector,
               lambda act, k, post: None, before_vector)


def load_layer3(nc, io, w, bias):
    with ExitStack() as ctx:
        loaded = ctx.enter_context(Semaphores(nc))("w3_loaded")
        with nc.Block() as blk:
            @blk.sync
            def _(sp):
                for i in range(2):
                    sp.dma_start(w[i][:], io[f"L3_gnn_W{i + 1}"]).then_inc(loaded, 16)
                    sp.dma_start(bias[i][:], io[f"L3_gnn_b{i + 1}"].rearrange("(a n) -> a n", a=1)
                                 .to_broadcast([NL, D])).then_inc(loaded, 16)
                sp.wait_ge(loaded, 64)


def build(nc, io, out):
    dram = lambda name, shape, dt: nc.dram_tensor(name, shape, dt, kind="Internal").ap()
    key_rows = dram("key_rows", [N_EDGES], I16)
    block_rows = dram("block_rows", [N_EDGES], BF16)
    sorted_rows = dram("sorted_rows", [N_SLOTS + SPILL_ROWS, ROW], F32)
    qkv_rows = dram("qkv_rows", [N_NODES, 3 * D], F32)
    weighted = dram("weighted", [NB, 128, NB, NL], F32)
    counts = dram("counts", [NB, 128, NB, 128], BF16)
    counts_t = dram("counts_t", [NB, 128, NB, 128], BF16)
    Semaphores.made = {}
    with ExitStack() as ctx:
        sb = lambda name, shape, dt, c=ctx: c.enter_context(nc.sbuf_tensor(name, shape, dt))
        n_spilled = sb("n_spilled", [TE, 1], I32)
        x = sb("x", [NL, NB, D], F32)
        ident = sb("ident", [128, 128], F32)
        ident16 = sb("ident16", [128, 128], BF16)
        iota1 = sb("iota1", [128, 128], BF16)
        node_sums = sb("node_sums", [NL, NB, D + 2], F32)
        with ExitStack() as graph:
            q_parts = sb("q_parts", [NL, NB, 3, D], BF16, graph)
            kv_parts = sb("kv_parts", [NL, NB, 3, 2 * D], BF16, graph)
            with ExitStack() as sorting:
                zeroed = sorting.enter_context(Semaphores(nc))("zeroed")
                zeros = sb("zeros", [128, NB // 2 * ROW], F32, sorting)
                tbl = sb("tbl", [NL, NT, 11], F32, sorting)
                prepare(nc, io, tbl, key_rows, block_rows, sorted_rows, zeros, zeroed)
                with ExitStack() as projecting:
                    w_qkv = sb("w_qkv", [D, 3 * D], F32, projecting)
                    qkv = sb("qkv", [NL, NB, 3 * D], F32, projecting)
                    load_tables(nc, io, x, w_qkv, ident, iota1, ident16)
                    project(nc, "qkv_of", x, w_qkv[:], qkv, ident, 3 * D)
                    split_qkv(nc, qkv, q_parts, kv_parts, qkv_rows)
                sort_edges(nc, io, tbl, key_rows, block_rows, sorted_rows, zeros, zeroed, n_spilled)
            acc = sb("acc", [NL, NB, MW], F32, graph)
            build_graph(nc, io, sorted_rows, q_parts, kv_parts, iota1, ident16, acc, weighted, counts, counts_t)
            y0_rows = dram("y0_rows", [NL * YB, D + 2], F32)
            y0 = sb("y0", [NL, NB * (D + 2)], F32, graph)
            spill_messages(nc, io, sorted_rows, qkv_rows, y0_rows, y0[:], n_spilled, ident)
            collect(nc, acc, y0[:], node_sums)
        full = [sb(name, [NL, NB, D], F32) for name in ("hh", "xs", "sums", "y_sb", "rest")]
        hh, xs, sums, y_sb, rest = full
        parts = sb("parts", [NL, NB, 3, D], BF16)
        dinv1, dis2, dinv3 = (sb(name, [NL, NB], F32) for name in ("dinv1", "dis2", "dinv3"))
        coeff = sb("coeff", [NL, 6], F32)
        w3 = [sb(f"w3_{i}", [D, D], F32) for i in range(2)]
        bias3 = [sb(f"bias3_{i}", [NL, D], F32) for i in range(2)]
        rows = dram("rows", [N_NODES, D], F32)
        y_rows = dram("y_rows", [NL * YB, D], F32)
        shared = (io, sorted_rows, rows, y_rows, n_spilled, ident)

        layer_norm(nc, "ln0", x, node_sums[:, :, 0:D], 1.0 / (8.0 ** 0.5 * 32.0), rest)
        scale_of_degree(nc, "dinv1", node_sums[:, :, D], 1.0, dinv1)
        scale_of_degree(nc, "dis2", node_sums[:, :, D + 1], 0.0, dis2)
        scale_of_degree(nc, "dinv3", node_sums[:, :, D + 1], 1.0, dinv3)
        smooth(nc, shared, x, hh, dinv1, xs, sums, y_sb, rest, weighted)
        layer_norm(nc, "ln1", x, hh[:], 1.0, rest)
        coefficients(nc, io, x, rest, coeff)
        polynomial(nc, shared, x, hh, dis2, coeff, xs, parts, sums, y_sb, rest, counts_t)
        layer_norm(nc, "ln2", x, hh[:], 1.0, rest)
        load_layer3(nc, io, w3, bias3)
        project(nc, "conv1_of", x, w3[0][:], hh, ident, D)
        convolve(nc, "conv1", shared, hh, bias3[0], True, dinv3, xs, parts, sums, y_sb, rest, counts)
        project(nc, "conv2_of", hh, w3[1][:], sums, ident, D)
        convolve(nc, "conv2", shared, sums, bias3[1], False, dinv3, xs, parts, hh, y_sb, rest, counts)
        layer_norm(nc, "ln3", x, sums[:], 1.0, rest, out_rows=out)


def kernel(**inputs):
    import numpy as np
    import concourse.bacc as bacc
    from concourse.bass_utils import run_bass_kernel_spmd

    a = {k.replace("L0_gnn_", ""): np.ascontiguousarray(v) for k, v in inputs.items()}
    cols = lambda v: np.ascontiguousarray(v.reshape(NT, TE).T)
    a["dst_cols"], a["src_cols"], a["weight_cols"] = cols(a["dst"]), cols(a["src"]), cols(a.pop("edge_weight"))
    a["attr16_t"] = np.ascontiguousarray(a.pop("edge_attr_16").T)
    a["attr8_t"] = np.ascontiguousarray(a.pop("edge_attr_8").T)
    a["L2_gnn_W1_t"], a["L2_gnn_W2_t"] = (np.ascontiguousarray(a[n].T) for n in ("L2_gnn_W1", "L2_gnn_W2"))
    a["iota"] = np.tile(np.arange(128, dtype=np.float32), (128, 1))
    a["lanes"] = np.arange(128, dtype=np.float32).reshape(128, 1)
    a["tri"] = np.tril(np.ones((128, 128), np.float32), -1)
    a["tri_t"] = np.triu(np.ones((128, 128), np.float32), 1)
    a["ident"] = np.eye(128, dtype=np.float32)

    nc = bacc.Bacc("TRN2", target_bir_lowering=False, num_devices=1)
    io = {n: nc.dram_tensor(f"in_{n}", v.shape, mybir.dt.from_np(v.dtype), kind="ExternalInput").ap()
          for n, v in a.items()}
    out = nc.dram_tensor("out", [N_NODES, D], F32, kind="ExternalOutput").ap()
    build(nc, io, out)
    r = run_bass_kernel_spmd(nc, [{f"in_{n}": v for n, v in a.items()}], core_ids=[0])
    return r.results[0]["out"]
```

```python
import concourse.bass as bass
from concourse import mybir
from contextlib import ExitStack, nullcontext
import numpy as np

F32, BF16, I32, I16, U8 = mybir.dt.float32, mybir.dt.bfloat16, mybir.dt.int32, mybir.dt.int16, mybir.dt.uint8
ALU, ACT, AX = mybir.AluOpType, mybir.ActivationFunctionType, mybir.AxisListType

N_NODES, D = 6250, 64
N_EDGES = 200000
NB = 50
NL = N_NODES // NB
TE = 125
NT = N_EDGES // TE
G = 8
NG = NT // G
CAP = 128
ROW = 72
DST_LANE, SRC_LANE, W1, ONE, DST, SRC = 64, 65, 66, 69, 70, 71
N_SLOTS = NB * CAP * NB
SPILL_ROWS = N_EDGES + 128
HID = 64


class Semaphores:
    made = {}

    def __init__(self, nc):
        self.nc, self.held = nc, []

    def __enter__(self):
        return self

    def __call__(self, name):
        if name not in self.made:
            self.made[name] = self.nc.alloc_semaphore(name=name)
        self.held.append(self.made[name])
        return self.made[name]

    def of_pool_dma(self, name):
        return self.nc.alloc_semaphore(name=name)

    def __exit__(self, *failure):
        with self.nc.Block() as blk:
            @blk.sync
            def _(sp):
                for held in self.held:
                    sp.sem_clear(held)


def prepare(nc, io, tbl, key_rows, block_rows, sorted_rows, zeros, zeroed):
    with ExitStack() as ctx:
        sb = lambda name, shape, dt: ctx.enter_context(nc.sbuf_tensor(f"prep_{name}", shape, dt))
        sem = ctx.enter_context(Semaphores(nc))
        ends = sb("ends", [NL, 2, NT], I32)
        node = sb("node", [NL, NT], F32)
        lane = sb("lane", [NL, NT], F32)
        block_d = sb("block_d", [NL, NT], F32)
        block_s = sb("block_s", [NL, NT], F32)
        weight = sb("weight", [NL, NT], F32)
        key16 = ends[:, 0, 0:NT // 2].bitcast(I16)
        block16 = sb("block16", [NL, NT], BF16)
        cols_in, rows_in, step = sem("cols_in"), sem("rows_in"), sem("step")
        cols_read, rows_ready, rows_out = sem("cols_read"), sem("rows_ready"), sem("rows_out")
        zeros_made = sem("zeros_made")
        with nc.Block() as blk:
            @blk.gpsimd
            def _(pool):
                pool.memset(zeros[:], 0.0).then_inc(zeros_made, 1)

            @blk.scalar
            def _(act):
                act.wait_ge(zeros_made, 1)
                view = sorted_rows[0:N_SLOTS, :].rearrange("(k b) c -> k (b c)", b=NB // 2)
                for b in range(2 * NB):
                    act.dma_start(view[b * CAP:(b + 1) * CAP, :], zeros[:]).then_inc(zeroed, 16)

            @blk.sync
            def _(sp):
                sp.dma_start(ends[:, 0, :], io["dst_cols"]).then_inc(cols_in, 16)
                sp.dma_start(ends[:, 1, :], io["src_cols"]).then_inc(cols_in, 16)
                sp.dma_start(weight[:], io["weight_cols"]).then_inc(cols_in, 16)
                sp.wait_ge(cols_read, 2)
                sp.dma_start(ends[:, 0, :], io["dst"].rearrange("(q c) -> q c", q=NL)).then_inc(rows_in, 16)
                sp.dma_start(ends[:, 1, :], io["src"].rearrange("(q c) -> q c", q=NL)).then_inc(rows_in, 16)
                sp.wait_ge(rows_ready, 1)
                sp.dma_start(key_rows.rearrange("(q c) -> q c", q=NL), key16).then_inc(rows_out, 16)
                sp.dma_start(block_rows.rearrange("(q c) -> q c", q=NL), block16[:]).then_inc(rows_out, 16)
                sp.wait_ge(rows_out, 32)

            @blk.vector
            def _(dve):
                n = [0]

                def link(ins):
                    n[0] += 1
                    ins.then_inc(step, 1)
                    dve.wait_ge(step, n[0])

                def split(which, block, read):
                    link(dve.tensor_copy(node[:], ends[:, which, :]))
                    if read:
                        dve.sem_inc(cols_read, 1)
                    link(dve.tensor_scalar(lane[:], node[:], 1.0 / NB, -0.49, ALU.mult, ALU.add))
                    link(dve.tensor_scalar(lane[:], lane[:], 12582912.0, None, ALU.add))
                    link(dve.tensor_scalar(lane[:], lane[:], 12582912.0, None, ALU.subtract))
                    link(dve.scalar_tensor_tensor(block[:], lane[:], -float(NB), node[:], ALU.mult, ALU.add))

                dve.wait_ge(cols_in, 48)
                split(0, block_d, True)
                link(dve.tensor_scalar(tbl[:, :, 0], lane[:], 1.0, None, ALU.add))
                link(dve.tensor_copy(tbl[:, :, 6], node[:]))
                split(1, block_s, True)
                link(dve.tensor_scalar(tbl[:, :, 1], lane[:], 1.0, None, ALU.add))
                link(dve.tensor_copy(tbl[:, :, 7], node[:]))
                rest = lane
                link(dve.tensor_copy(block16[:], weight[:]))
                link(dve.tensor_copy(tbl[:, :, 2], block16[:]))
                link(dve.tensor_tensor(rest[:], weight[:], block16[:], ALU.subtract))
                link(dve.tensor_copy(block16[:], rest[:]))
                link(dve.tensor_copy(tbl[:, :, 3], block16[:]))
                link(dve.tensor_tensor(tbl[:, :, 4], rest[:], block16[:], ALU.subtract))
                link(dve.tensor_scalar(tbl[:, :, 5], weight[:], 0.0, 1.0, ALU.mult, ALU.add))
                link(dve.tensor_copy(tbl[:, :, 8], weight[:]))
                link(dve.tensor_copy(tbl[:, :, 9], block_d[:]))
                link(dve.tensor_copy(tbl[:, :, 10], block_s[:]))
                dve.wait_ge(rows_in, 32)
                split(0, block_d, False)
                split(1, block_s, False)
                link(dve.tensor_copy(block16[:], block_d[:]))
                dve.scalar_tensor_tensor(key16, block_d[:], float(NB), block_s[:], ALU.mult, ALU.add)\
                   .then_inc(rows_ready, 1)


def sort_edges(nc, io, tbl, key_rows, block_rows, sorted_rows, zeros, zeroed, n_spilled):
    with ExitStack() as ctx:
        sb = lambda name, shape, dt: ctx.enter_context(nc.sbuf_tensor(f"sort_{name}", shape, dt))
        pb = lambda name, shape: ctx.enter_context(nc.psum_tensor(f"sort_{name}", shape, F32))
        sem = ctx.enter_context(Semaphores(nc))
        two = range(2)
        iota_blocks = sb("iota_blocks", [TE, NB], F32)
        tri = sb("tri", [TE, 2, TE], F32)
        before = sb("before", [TE, 2, TE], BF16)
        ones = sb("ones", [TE, TE], BF16)
        w1 = sb("w1", [24, 128], F32)
        b1 = sb("b1", [128, 1], F32)
        w2 = sb("w2", [128, D], F32)
        b2 = sb("b2", [TE, 3, D], F32)
        key_row = [sb(f"key_row{u}", [TE, G * TE], I16) for u in two]
        block_row = [sb(f"block_row{u}", [NB, G * TE], BF16) for u in two]
        attrs = [sb(f"attrs{u}", [24, G * TE], F32) for u in two]
        grp = [sb(f"grp{u}", [TE, G, 13], F32) for u in two]
        hot_d = [sb(f"hot_d{u}", [TE, G, NB], BF16) for u in two]
        hot_s = [sb(f"hot_s{u}", [TE, G, NB], BF16) for u in two]
        hot_dt = [sb(f"hot_dt{u}", [NB, G * TE], BF16) for u in two]
        hidden = [sb(f"hidden{u}", [128, G * TE], F32) for u in two]
        count = [sb(f"count{u}", [NB, NB], BF16) for u in two]
        same = sb("same", [TE, G, TE], BF16)
        picked = sb("picked", [TE, G, NB], F32)
        rank_in = sb("rank_in", [TE, G], F32)
        base = sb("base", [TE, G], F32)
        rank = sb("rank", [TE, G], F32)
        slot_row = sb("slot_row", [TE, G], F32)
        spills = sb("spills", [TE, G], BF16)
        spill_ps = sb("spill_ps", [TE, 2, G], F32)
        one_cols = sb("one_cols", [TE, G], F32)
        upto = sb("upto", [TE, G], F32)
        spill_row = sb("spill_row", [TE, G], F32)
        so_far = sb("so_far", [TE, 1], F32)
        biased = sb("biased", [TE, G, D], F32)
        rows = [sb(f"rows{u}", [TE, G, ROW], F32) for u in two]
        row_at = [sb(f"row_at{u}", [TE, G], I32) for u in two]
        pad_f = sb("pad_f", [TE, 1], F32)
        pad_at = sb("pad_at", [TE, 1], I32)
        lane_col = sb("lane_col", [TE, 1], F32)
        ps_h = [pb(f"ps_h{i}", [128, 512]) for i in two]
        ps_c = pb("ps_c", [128, 512])
        ps_r = [pb(f"ps_r{u}", [128, 512]) for u in two]
        ps_m = [pb(f"ps_m{u}", [128, 512]) for u in two]
        ps_f = pb("ps_f", [128, 512])

        const_in, made = sem("const_in"), sem("made")
        loaded = [sem(f"loaded{u}") for u in two]
        step, hots, rows_read, hidden_ps = sem("step"), sem("hots"), sem("rows_read"), sem("hidden_ps")
        silu, counted, snapped, based = sem("silu"), sem("counted"), sem("snapped"), sem("based")
        mixed, flagged, prefixed, rows_ready = sem("mixed"), sem("flagged"), sem("prefixed"), sem("rows_ready")
        stored = [sem.of_pool_dma(f"row_stored{u}") for u in two]
        padded, taken = sem.of_pool_dma("padded"), sem("taken")
        H = G // 2
        N_CONST = 16 * 12

        with nc.Block() as blk:
            @blk.sync
            def _(sp):
                for dst, src in ((iota_blocks[:], io["iota"][0:TE, 0:NB]), (lane_col[:], io["lanes"][0:TE, :]),
                                 (tri[:, 0, :], io["tri"][0:TE, 0:TE]), (tri[:, 1, :], io["tri_t"][0:TE, 0:TE]),
                                 (b1[0:HID, :], io["b_sph1"].rearrange("(p a) -> p a", a=1)),
                                 (b1[HID:128, :], io["b_rad1"].rearrange("(p a) -> p a", a=1)),
                                 (w2[0:HID, :], io["W_sph2"]), (w2[HID:128, :], io["W_rad2"]),
                                 (b2[:, 0, :], io["b_sph2"].rearrange("(a n) -> a n", a=1).to_broadcast([TE, D])),
                                 (b2[:, 1, :], io["b_rad2"].rearrange("(a n) -> a n", a=1).to_broadcast([TE, D]))):
                    sp.dma_start(dst, src).then_inc(const_in, 16)
                sp.wait_ge(made, 1)
                sp.dma_start(w1[0:16, 0:HID], io["W_sph1"]).then_inc(const_in, 16)
                sp.dma_start(w1[16:24, HID:128], io["W_rad1"]).then_inc(const_in, 16)

                def loads(u, edges):
                    sp.dma_start(key_row[u][:], key_rows[edges].rearrange("(a n) -> a n", a=1)
                                 .to_broadcast([TE, G * TE])).then_inc(loaded[u], 16)
                    sp.dma_start(block_row[u][:], block_rows[edges].rearrange("(a n) -> a n", a=1)
                                 .to_broadcast([NB, G * TE])).then_inc(loaded[u], 16)
                    sp.dma_start(attrs[u][0:16, :], io["attr16_t"][:, edges]).then_inc(loaded[u], 16)
                    sp.dma_start(attrs[u][16:24, :], io["attr8_t"][:, edges]).then_inc(loaded[u], 16)

                for u in two:
                    loads(u, slice(u * G * TE, (u + 1) * G * TE))
                with sp.Fori(0, NG // 2 - 1) as it:
                    for u in two:
                        sp.wait_ge(rows_read, 2 * it + (u + 1))
                        sp.sem_inc(taken, 1)
                        sp.wait_ge(hidden_ps, 4 * it + (2 * u + 2))
                        sp.sem_inc(taken, 1)
                        loads(u, bass.ds((2 * it + (2 + u)) * (G * TE), G * TE))

            @blk.gpsimd
            def _(pool):
                pool.memset(w1[:], 0.0).then_inc(made, 1)
                for u in two:
                    pool.memset(rows[u][:], 0.0)
                pool.memset(one_cols[:], 1.0)
                pool.memset(so_far[:], 0.0)
                pool.memset(count[0][:], 0.0)
                pool.memset(ones[:], 1.0).then_inc(made, 1)
                pool.wait_ge(zeroed, 32 * NB)

                with pool.Fori(0, NG // 2) as it:
                    for u in two:
                        pool.wait_ge(rows_ready, 2 * it + (u + 1))
                        pool.sem_inc(taken, 1)
                        for j in range(G):
                            pool.indirect_dma_start(
                                out=sorted_rows, out_offset=bass.IndirectOffsetOnAxis(row_at[u][:, j:j + 1], 0),
                                in_=rows[u][:, j, :], in_offset=None,
                                bounds_check=N_SLOTS + SPILL_ROWS - 1, oob_is_err=False).then_inc(stored[u], 16)
                pool.wait_ge(rows_ready, NG + 1)
                pool.indirect_dma_start(
                    out=sorted_rows, out_offset=bass.IndirectOffsetOnAxis(pad_at[:, 0:1], 0),
                    in_=zeros[0:TE, 0:ROW], in_offset=None,
                    bounds_check=N_SLOTS + SPILL_ROWS - 1, oob_is_err=False).then_inc(padded, 16)
                for u in two:
                    pool.wait_ge(stored[u], 16 * G * (NG // 2))
                pool.wait_ge(padded, 16)

            @blk.scalar
            def _(act):
                act.wait_ge(const_in, N_CONST)

                def group(n, first):
                    u = 1 if first == 1 else n[1]
                    n = n[0]
                    for j in range(G):
                        if j in (1, 3):
                            h = j // 2
                            act.wait_ge(hidden_ps, 2 * n + (h + 1))
                            if h == 0 and first is None:
                                act.wait_ge(mixed, n - 1)
                            act.activation(hidden[u][:, h * H * TE:(h + 1) * H * TE], ps_h[h][:, 0:H * TE],
                                           ACT.Silu, bias=b1[:, 0:1]).then_inc(silu, 1)
                        act.wait_ge(counted, n * G + (j + 1))
                        act.activation(count[(j + 1) % 2][:], ps_c[0:NB, 0:NB], ACT.Copy).then_inc(snapped, 1)

                group((0, 0), 0)
                group((1, 1), 1)
                with act.Fori(1, NG // 2) as it:
                    for u in two:
                        group((2 * it + u, u), None)

            @blk.tensor
            def _(pe):
                pe.wait_ge(made, 2)
                pe.wait_ge(const_in, N_CONST)
                nc.tensor.matmul(ps_c[0:NB, 0:NB], count[0][:], count[0][:], start=True, stop=True,
                                 skip_group_check=True)

                def group(n, it, u, first):
                    pe.wait_ge(loaded[u], 64 * it + 64)

                    def hidden_layer(h):
                        if first != 0:
                            pe.wait_ge(silu, 2 * n + (h - 1))
                        nc.tensor.matmul(ps_h[h][:, 0:H * TE], w1[:], attrs[u][:, h * H * TE:(h + 1) * H * TE],
                                         start=True, stop=True).then_inc(hidden_ps, 1)
                    hidden_layer(0)
                    pe.wait_ge(hots, n + 1)
                    for j in range(G):
                        if not (first == 0 and j == 0):
                            pe.wait_ge(snapped, n * G + j)
                        last = nc.tensor.matmul(ps_r[u][0:TE, j * NB:(j + 1) * NB], hot_dt[u][:, j * TE:(j + 1) * TE],
                                                count[j % 2][:], start=True, stop=True, skip_group_check=True)
                        if j == G - 1:
                            last.then_inc(based, 1)
                        nc.tensor.matmul(ps_c[0:NB, 0:NB], hot_d[u][:, j, :], hot_s[u][:, j, :], start=False,
                                         stop=True, skip_group_check=True).then_inc(counted, 1)
                        if j == 0:
                            hidden_layer(1)
                        if j == 1 and first != 0:
                            prefixes(n)
                        if j == H:
                            pe.wait_ge(silu, 2 * n + 2)
                        if j >= H:
                            for t in (2 * (j - H), 2 * (j - H) + 1):
                                last = nc.tensor.matmul(ps_m[u][0:TE, t * D:(t + 1) * D],
                                                        hidden[u][:, t * TE:(t + 1) * TE], w2[:], start=True,
                                                        stop=True, skip_group_check=True)
                    last.then_inc(mixed, 1)

                def prefixes(n):
                    pe.wait_ge(flagged, n)
                    nc.tensor.matmul(ps_f[0:TE, 0:G], before[:, 1, :], spills[:], start=True, stop=True,
                                     skip_group_check=True)
                    nc.tensor.matmul(ps_f[0:TE, G:2 * G], ones[:], spills[:], start=True, stop=True,
                                     skip_group_check=True).then_inc(prefixed, 1)

                group(0, 0, 0, 0)
                group(1, 0, 1, 1)
                with pe.Fori(1, NG // 2) as it:
                    for u in two:
                        group(2 * it + u, it, u, None)
                prefixes(NG)

            @blk.vector
            def _(dve):
                dve.wait_ge(const_in, N_CONST)
                dve.wait_ge(made, 2)
                dve.tensor_tensor(b2[:, 2, :], b2[:, 0, :], b2[:, 1, :], ALU.add)
                dve.tensor_copy(before[:], tri[:])

                def group_hots(g, it, u, first):
                    g_is_0 = isinstance(g, int) and g == 0
                    dve.wait_ge(loaded[u], 64 * it + 64)
                    if not first:
                        dve.wait_ge(mixed, g - 1)
                    dve.tensor_copy(grp[u][:, :, 0:11], tbl[:, bass.ds(g * G, G), :]).then_inc(step, 1)
                    dve.wait_ge(step, 1 if g_is_0 else STEPS * g - (STEPS - 2))
                    dve.scalar_tensor_tensor(grp[u][:, :, 11], grp[u][:, :, 9], float(NB), grp[u][:, :, 10],
                                             ALU.mult, ALU.add)
                    dve.scalar_tensor_tensor(grp[u][:, :, 12], grp[u][:, :, 9], float(NB * CAP), grp[u][:, :, 10],
                                             ALU.mult, ALU.add)
                    iota3 = iota_blocks[:].unsqueeze(1).to_broadcast([TE, G, NB])
                    dve.tensor_tensor(hot_d[u][:], iota3, grp[u][:, :, 9:10].to_broadcast([TE, G, NB]), ALU.is_equal)
                    dve.tensor_tensor(hot_s[u][:], iota3, grp[u][:, :, 10:11].to_broadcast([TE, G, NB]), ALU.is_equal)
                    dve.tensor_scalar(hot_dt[u][:], block_row[u][:], lane_col[0:NB, 0:1], None,
                                      ALU.is_equal).then_inc(hots, 1)

                def link(ins, value):
                    ins.then_inc(step, 1)
                    dve.wait_ge(step, value)

                STEPS = 12

                def places(g, it, u, done):
                    at = STEPS * g + 2 if done else STEPS * g + 1
                    k = [0]

                    def nxt(ins):
                        k[0] += 1
                        link(ins, at + k[0])
                    for j in range(G):
                        last = dve.scalar_tensor_tensor(same[:, j, :], key_row[u][:, j * TE:(j + 1) * TE],
                                                        grp[u][:, j, 11:12], before[:, 0, :], ALU.is_equal, ALU.mult,
                                                        accum_out=rank_in[:, j:j + 1])
                    last.then_inc(rows_read, 1)
                    dve.wait_ge(rows_read, g + 1)
                    dve.wait_ge(based, g + 1)
                    nxt(dve.tensor_tensor(picked[:], ps_r[u][0:TE, 0:G * NB].rearrange("p (g b) -> p g b", g=G),
                                          hot_s[u][:], ALU.mult))
                    nxt(dve.tensor_reduce(base[:], picked[:], AX.X, ALU.add))
                    nxt(dve.tensor_tensor(rank[:], rank_in[:], base[:], ALU.add))
                    dve.tensor_scalar(spills[:], rank[:], float(CAP), None, ALU.is_ge).then_inc(flagged, 1)
                    nxt(dve.scalar_tensor_tensor(slot_row[:], rank[:], float(NB), grp[u][:, :, 12], ALU.mult, ALU.add))
                    dve.wait_ge(mixed, g + 1)
                    dve.wait_ge(stored[u], 16 * G * it)
                    nxt(dve.tensor_tensor(biased[:], ps_m[u][0:TE, :].rearrange("p (g d) -> p g d", g=G),
                                          b2[:, 2:3, :].to_broadcast([TE, G, D]), ALU.add))
                    dve.tensor_tensor(rows[u][:, :, 0:D], biased[:], grp[u][:, :, 8:9].to_broadcast([TE, G, D]), ALU.mult)
                    dve.tensor_copy(rows[u][:, :, D:ROW], grp[u][:, :, 0:8])
                    dve.wait_ge(prefixed, g + 1)
                    nxt(dve.tensor_copy(spill_ps[:], ps_f[0:TE, 0:2 * G].rearrange("p (a g) -> p a g", a=2)))
                    nxt(dve.tensor_tensor_scan(upto[:], one_cols[:], spill_ps[:, 1, :], so_far[:, 0:1],
                                               ALU.mult, ALU.add))
                    dve.tensor_copy(so_far[:], upto[:, G - 1:G])
                    nxt(dve.tensor_tensor(spill_row[:], spill_ps[:, 0, :], spill_ps[:, 1, :], ALU.subtract))
                    nxt(dve.tensor_tensor(spill_row[:], spill_row[:], upto[:], ALU.add))
                    nxt(dve.scalar_tensor_tensor(spill_row[:], spill_row[:], float(N_SLOTS), slot_row[:],
                                                 ALU.add, ALU.subtract))
                    nxt(dve.tensor_tensor(spill_row[:], spill_row[:], spills[:], ALU.mult))
                    dve.tensor_tensor(row_at[u][:], spill_row[:], slot_row[:], ALU.add).then_inc(rows_ready, 1)
                    assert k[0] == STEPS - 1

                group_hots(0, 0, 0, True)
                group_hots(1, 0, 1, True)
                places(0, 0, 0, 1)
                with dve.Fori(1, NG // 2) as it:
                    group_hots(2 * it, it, 0, False)
                    places(2 * it - 1, it - 1, 1, 1)
                    group_hots(2 * it + 1, it, 1, False)
                    places(2 * it, it, 0, 1)
                places(NG - 1, NG // 2 - 1, 1, 0)
                at = STEPS * NG
                link(dve.tensor_scalar(pad_f[:], lane_col[:], so_far[:, 0:1], float(N_SLOTS), ALU.add, ALU.add), at + 1)
                dve.tensor_copy(pad_at[:], pad_f[:]).then_inc(rows_ready, 1)
                dve.wait_ge(rows_ready, NG + 1)
                link(dve.tensor_scalar(pad_f[:], so_far[:], 1.0 / TE, -0.496, ALU.mult, ALU.add), at + 2)
                link(dve.tensor_scalar(pad_f[:], pad_f[:], 12582912.0, None, ALU.add), at + 3)
                link(dve.tensor_scalar(pad_f[:], pad_f[:], 12582911.0, None, ALU.subtract), at + 4)
                dve.tensor_copy(n_spilled[:], pad_f[:])



def project(nc, tag, x, weights, out, ident, n_out):
    with ExitStack() as ctx:
        sb = lambda name, shape, dt: ctx.enter_context(nc.sbuf_tensor(f"{tag}_{name}", shape, dt))
        pb = lambda name, shape: ctx.enter_context(nc.psum_tensor(f"{tag}_{name}", shape, F32))
        sem = ctx.enter_context(Semaphores(nc))
        two = range(2)
        block = [sb(f"block{u}", [NL, D], F32) for u in two]
        block_t = [sb(f"block_t{u}", [D, NL], F32) for u in two]
        ps_t = [pb(f"ps_t{u}", [128, 512]) for u in two]
        ps_o = [pb(f"ps_o{u}", [128, 512]) for u in two]
        taken = sem("taken")
        staged, turned, turned_sb, product, kept = (sem(n) for n in ("staged", "turned", "turned_sb", "product", "kept"))
        with nc.Block() as blk:
            @blk.scalar
            def _(act):
                act.sem_inc(turned, 2)
                act.sem_inc(product, 2)
                with act.Fori(0, NB // 2) as it:
                    for u in two:
                        act.wait_ge(turned, 2 * it + (u + 1))
                        act.activation(block[u][:], x[:, bass.ds(2 * it + u, 1), :].rearrange("p a d -> p (a d)"),
                                       ACT.Copy).then_inc(staged, 1)
                    for u in two:
                        act.wait_ge(turned, 2 * it + (u + 3))
                        act.wait_ge(product, 2 * it + (u + 1))
                        act.activation(block_t[u][:], ps_t[u][0:D, 0:NL], ACT.Copy).then_inc(turned_sb, 1)

            @blk.tensor
            def _(pe):
                pe.sem_inc(kept, 2)
                with pe.Fori(0, NB // 2) as it:
                    for u in two:
                        pe.wait_ge(staged, 2 * it + (u + 1))
                        pe.sem_inc(taken, 1)
                        nc.tensor.transpose(ps_t[u][0:D, 0:NL], block[u][:], ident[0:NL, 0:NL]).then_inc(turned, 1)
                    for u in two:
                        pe.wait_ge(turned_sb, 2 * it + (u + 1))
                        pe.wait_ge(kept, 2 * it + (u + 1))
                        nc.tensor.matmul(ps_o[u][0:NL, 0:n_out], block_t[u][:], weights, start=True,
                                         stop=True).then_inc(product, 1)

            @blk.vector
            def _(dve):
                with dve.Fori(0, NB // 2) as it:
                    for u in two:
                        dve.wait_ge(product, 2 * it + (u + 3))
                        dve.tensor_copy(out[:, bass.ds(2 * it + u, 1), :].rearrange("p a d -> p (a d)"),
                                        ps_o[u][0:NL, 0:n_out]).then_inc(kept, 1)


def load_tables(nc, io, x, w_qkv, ident, iota1, ident16):
    with ExitStack() as ctx:
        loaded = ctx.enter_context(Semaphores(nc))("tables_loaded")
        iota_f = ctx.enter_context(nc.sbuf_tensor("iota_f", [128, 128], F32))
        with nc.Block() as blk:
            @blk.sync
            def _(sp):
                sp.dma_start(x[:], io["x"].rearrange("(p b) d -> p b d", b=NB)).then_inc(loaded, 16)
                for i, name in enumerate(("Wq", "Wk", "Wv")):
                    sp.dma_start(w_qkv[:, i * D:(i + 1) * D], io[name]).then_inc(loaded, 16)
                sp.dma_start(ident[:], io["ident"]).then_inc(loaded, 16)
                sp.dma_start(iota_f[:], io["iota"]).then_inc(loaded, 16)
                sp.wait_ge(loaded, 96)

            @blk.vector
            def _(dve):
                dve.wait_ge(loaded, 96)
                dve.tensor_scalar(iota1[:], iota_f[:], 1.0, None, ALU.add)
                dve.tensor_copy(ident16[:], ident[:])


def split_qkv(nc, qkv, q_parts, kv_parts, qkv_rows):
    with ExitStack() as ctx:
        sem = ctx.enter_context(Semaphores(nc))
        step, out = sem("step"), sem("qkv_out")
        with nc.Block() as blk:
            @blk.sync
            def _(sp):
                sp.dma_start(qkv_rows.rearrange("(p b) d -> p (b d)", b=NB), qkv[:].rearrange("p b d -> p (b d)"))\
                  .then_inc(out, 16)
                sp.wait_ge(out, 16)

            @blk.vector
            def _(dve):
                n = [0]

                def link(ins):
                    n[0] += 1
                    ins.then_inc(step, 1)
                    dve.wait_ge(step, n[0])

                def split(parts, whole):
                    for i in range(2):
                        link(dve.tensor_copy(parts[:, :, i, :], whole))
                        link(dve.tensor_tensor(whole, whole, parts[:, :, i, :], ALU.subtract))
                    dve.tensor_copy(parts[:, :, 2, :], whole)

                dve.wait_ge(out, 16)
                split(q_parts, qkv[:, :, 0:D])
                split(kv_parts, qkv[:, :, D:3 * D])


NP = 10
HP = NP // 2
N_HG, N_RP = NB // NP, NB // 2
MW = 3 * D + 4


def build_graph(nc, io, sorted_rows, q_parts, kv_parts, iota1, ident16, acc, weighted, counts, counts_t):
    LOOK, WEIGH, MESSAGE, PART0, REST, PART1, PART2, SUM = 1, 2, 2, 3, 4, 5, 6, 7
    with ExitStack() as ctx:
        sb = lambda name, shape, dt: ctx.enter_context(nc.sbuf_tensor(f"graph_{name}", shape, dt))
        pb = lambda name, shape, dt=F32: ctx.enter_context(nc.psum_tensor(f"graph_{name}", shape, dt))
        sem = ctx.enter_context(Semaphores(nc))
        two, five = range(2), range(5)
        edges = [sb(f"edges{h}", [128, 2, HP, ROW], F32) for h in two]
        hot = [sb(f"hot{b}", [128, 2, 2, 128], BF16) for b in range(NP)]
        heavy = [sb(f"heavy{b}", [128, 2, 3, 128], BF16) for b in five]
        hot_t = [sb(f"hot_t{u}", [128, 2, 2, 128], BF16) for u in two]
        qw = sb("qw", [128, 2, D], F32)
        qwk = sb("qwk", [128, 2, D], F32)
        alpha = sb("alpha", [128, 16], F32)
        msg = [sb(f"msg{b}", [128, 2, D], F32) for b in five]
        rest = [sb(f"rest{b}", [128, 2, D], F32) for b in five]
        parts = [sb(f"parts{b}", [128, 2, MW], BF16) for b in range(NP)]
        st_w = [sb(f"st_w{h}", [128, 2, HP, NL], F32) for h in two]
        st_c = [sb(f"st_c{h}", [128, 2, HP, 128], U8) for h in two]
        st_t = [sb(f"st_t{h}", [128, HP, 2, 128], U8) for h in two]
        none = sb("none", [128, 2 * MW], BF16)
        ps_t = [pb(f"ps_t{u}", [128, 2, 2, 256], BF16) for u in two]
        ps_w = pb("ps_w", [128, 4, 128])
        ps_c = [pb(f"ps_c{u}", [128, 2, 2, 128]) for u in two]
        ps_l = [pb(f"ps_l{u}", [128, 512]) for u in two]
        ps_o = pb("ps_o", [128, 512])

        loaded = [sem(f"loaded{h}") for h in two]
        stored = [sem(f"stored{h}") for h in two]
        cleared, hots, heavies, columns = sem("cleared"), sem("hots"), sem("heavies"), sem("columns")
        turned, turned_sb, blocks, blocks_sb = sem("turned"), sem("turned_sb"), sem("blocks"), sem("blocks_sb")
        weighed, weights_sb, looked, msgs = sem("weighed"), sem("weights_sb"), sem("looked"), sem("msgs")
        part0, rests, part1, split = sem("part0"), sem("rests"), sem("part1"), sem("split")
        summed, added, step, taken = sem("summed"), sem("sums_added"), sem("step"), sem("taken")
        B_SUMMED, B_BLOCKS_SB, B_WEIGHTS_SB, B_LOOKED, B_MSGS = NP, 2, 1, 2, 5
        B_WEIGHED, B_SPLIT, B_TAKEN = 5, 5, 2
        by_slot = sorted_rows[0:N_SLOTS, :].rearrange("(h r s) c -> h r s c", r=CAP, s=NB)

        def steps(eng, body):
            body(0, 0, 0, "first")
            with eng.Fori(1, N_HG) as hg:
                body(0, hg, hg, "src")
            with eng.Fori(1, N_RP) as rp:
                body(rp, 0, rp * N_HG, "dst")
                with eng.Fori(1, N_HG) as hg:
                    body(rp, hg, rp * N_HG + hg, "src")

        def pairs(s, lag, at):
            return [s - lag] if s >= lag or at != "first" else []

        with nc.Block() as blk:
            @blk.sync
            def _(sp):
                def body(rp, hg, n, at):
                    for h in two:
                        if at != "first":
                            for used in (msgs, heavies, columns):
                                sp.wait_ge(used, (n - 1) * NP + (HP * h + HP + (B_MSGS if used is msgs else 0)))
                                sp.sem_inc(taken, 1)
                        d0, s0 = (bass.ds(2 * rp, 2), bass.ds(hg * NP + HP * h, HP)) if at != "first" else \
                            (slice(0, 2), slice(HP * h, HP * h + HP))
                        sp.dma_start(edges[h][:].rearrange("r h s c -> r h (s c)"),
                                     by_slot[d0, :, s0, :].rearrange("h r s c -> r h (s c)")).then_inc(loaded[h], 16)
                steps(sp, body)

            @blk.gpsimd
            def _(pool):
                pool.memset(acc[:], 0.0)
                pool.memset(none[:], 0.0).then_inc(cleared, 1)

                def body(rp, hg, n, at):
                    for s in range(NP):
                        h, k = s // HP, s % HP
                        pool.wait_ge(hots, n * NP + (s + 1))
                        pool.wait_ge(weighed, n * NP + (s + 1))
                        pool.sem_inc(taken, 1)
                        pool.tensor_tensor(heavy[s % 5][:], hot[s][:, :, 0:1].to_broadcast([128, 2, 3, 128]),
                                           edges[h][:, :, k, W1:W1 + 3].unsqueeze(3).to_broadcast([128, 2, 3, 128]),
                                           ALU.mult).then_inc(heavies, 1)
                        pool.wait_ge(summed, n * NP + (s + 1))
                        pool.sem_inc(taken, 1)
                        pool.tensor_copy(parts[s][:, :, 3 * D:MW], edges[h][:, :, k, W1:W1 + 4]).then_inc(columns, 1)
                steps(pool, body)

            @blk.scalar
            def _(act):
                act.sem_inc(blocks_sb, B_BLOCKS_SB)
                act.sem_inc(weights_sb, B_WEIGHTS_SB)

                def stores(h, rp, hg, n):
                    act.wait_ge(blocks_sb, n * NP + (HP * h + HP + B_BLOCKS_SB))
                    act.wait_ge(weights_sb, n * NP + (HP * h + HP + B_WEIGHTS_SB))
                    s0, d0 = bass.ds(hg * NP + HP * h, HP), bass.ds(2 * rp, 2)
                    act.dma_start(weighted[d0, :, s0, :].rearrange("h p s d -> p h (s d)"),
                                  st_w[h][:].rearrange("p h s d -> p h (s d)")).then_inc(stored[h], 16)
                    act.dma_start(counts[d0, :, s0, :].rearrange("h p s d -> p h (s d)"),
                                  st_c[h][:].rearrange("p h s d -> p h (s d)")).then_inc(stored[h], 16)
                    act.dma_start(counts_t[s0, :, d0, :].rearrange("s p h d -> p s (h d)"),
                                  st_t[h][:].rearrange("p s h d -> p s (h d)")).then_inc(stored[h], 16)

                def weights_out(r, n):
                    act.wait_ge(weighed, n * NP + (r + 1 + B_WEIGHED))
                    act.activation(st_w[(r % NP) // HP][:, :, r % HP, :], ps_w[:, 0:2, 0:NL],
                                   ACT.Copy).then_inc(weights_sb, 1)

                def part_0(r, n):
                    act.wait_ge(msgs, n * NP + (r + 1 + B_MSGS))
                    act.activation(parts[r % NP][:, :, 0:D], msg[r % 5][:], ACT.Copy).then_inc(part0, 1)

                def part_1(r, n):
                    act.wait_ge(rests, n * NP + (r + 1))
                    act.activation(parts[r % NP][:, :, D:2 * D], rest[r % 5][:], ACT.Copy).then_inc(part1, 1)

                def body(rp, hg, n, at):
                    before = {"first": None, "src": (rp, hg - 1), "dst": (rp - 1, N_HG - 1)}[at]
                    for s in range(NP):
                        u, h, k = s % 2, s // HP, s % HP
                        for r in pairs(s, PART0, at):
                            part_0(r, n)
                        for r in pairs(s, PART1, at):
                            part_1(r, n)
                        act.wait_ge(turned, n * NP + (s + 1))
                        if not (at == "first" and s < 2):
                            act.wait_ge(looked, n * NP + (s - 2 + 1 + B_LOOKED))
                        act.activation(hot_t[u][:], ps_t[u][:, :, :, 0:128], ACT.Copy).then_inc(turned_sb, 1)
                        act.wait_ge(blocks, n * NP + (s + 1))
                        if k == 0 and at != "first":
                            act.wait_ge(stored[h], 48 * n)
                        act.activation(st_c[h][:, :, k, :], ps_c[u][:, 0], ACT.Copy)
                        act.activation(st_t[h][:, k, :, :], ps_c[u][:, 1], ACT.Copy).then_inc(blocks_sb, 1)
                        for r in pairs(s, WEIGH, at):
                            weights_out(r, n)
                            if r == -1:
                                stores(1, *before, n - 1)
                            if r == HP - 1:
                                stores(0, rp, hg, n)
                steps(act, body)
                n = N_HG * N_RP
                for s in range(SUM):
                    for lag, stage in ((WEIGH, weights_out), (PART0, part_0), (PART1, part_1)):
                        if s < lag:
                            stage(s - lag, n)
                stores(1, N_RP - 1, N_HG - 1, n - 1)
                for h in two:
                    act.wait_ge(stored[h], 48 * n)

            @blk.tensor
            def _(pe):
                pe.sem_inc(summed, B_SUMMED)
                pe.sem_inc(looked, B_LOOKED)
                pe.sem_inc(weighed, B_WEIGHED)
                pe.wait_ge(cleared, 1)

                def look_up(r, n, rp, hg, at):
                    u = r % 2
                    if at == "dst" and r < 0:
                        src, dst = NB + r, 2 * (rp - 1)
                    else:
                        src, dst = hg * NP + r, 2 * rp
                    rows = lambda table, b: (table[:, bass.ds(b, 1)] if not isinstance(b, int) else table[:, b:b + 1])
                    flat = lambda a, i: a[:, :, i].rearrange("p a d -> p (a d)")
                    pe.wait_ge(turned_sb, n * NP + (r + 1))
                    if not (at == "first" and r < 2):
                        pe.wait_ge(msgs, n * NP + (r - 2 + 1 + B_MSGS))
                    for t in two:
                        for i in range(3):
                            nc.tensor.matmul(ps_l[u][:, t * 2 * D:(t + 1) * 2 * D], hot_t[u][0:NL, t, 1],
                                             flat(rows(kv_parts, src), i), start=i == 0, stop=i == 2,
                                             skip_group_check=True)
                        for i in range(3):
                            last = nc.tensor.matmul(ps_l[u][:, (4 + t) * D:(5 + t) * D], hot_t[u][0:NL, t, 0],
                                                    flat(rows(q_parts, dst + t), i), start=i == 0, stop=i == 2,
                                                    skip_group_check=True)
                    last.then_inc(looked, 1)

                def weigh(r, n):
                    pe.wait_ge(heavies, n * NP + (r + 1))
                    pe.wait_ge(weights_sb, n * NP + (r + B_WEIGHTS_SB))
                    for t in two:
                        for i in range(3):
                            last = nc.tensor.matmul(ps_w[:, t], hot[r % NP][:, t, 1], heavy[r % 5][:, t, i],
                                                    start=i == 0, stop=i == 2, skip_group_check=True)
                    last.then_inc(weighed, 1)

                def clear_sums():
                    nc.tensor.matmul(ps_o[:, 0:2 * MW], none[:, 0:128], none[:], start=True, stop=True,
                                     skip_group_check=True)

                def add_up(r, n):
                    pe.wait_ge(split, n * NP + (r + 1 + B_SPLIT))
                    pe.wait_ge(columns, n * NP + (r + 1))
                    for t in two:
                        last = nc.tensor.matmul(ps_o[:, t * MW:(t + 1) * MW], hot[r % NP][:, t, 0], parts[r % NP][:, t],
                                                start=False, stop=True, skip_group_check=True)
                    last.then_inc(summed, 1)

                clear_sums()

                def body(rp, hg, n, at):
                    for s in range(NP):
                        u = s % 2
                        pe.wait_ge(hots, n * NP + (s + 1))
                        if not (at == "first" and s < 2):
                            pe.wait_ge(turned_sb, n * NP + (s - 1))
                        for t in two:
                            for w in two:
                                last = nc.tensor.transpose(ps_t[u][:, t, w, 0:128], hot[s][:, t, w], ident16[:])
                        last.then_inc(turned, 1)
                        pe.wait_ge(blocks_sb, n * NP + (s + 1))
                        for t in two:
                            dst, src = hot[s][:, t, 0], hot[s][:, t, 1]
                            nc.tensor.matmul(ps_c[u][:, 1, t], dst, src, start=True, stop=True, skip_group_check=True)
                            last = nc.tensor.matmul(ps_c[u][:, 0, t], src, dst, start=True, stop=True,
                                                    skip_group_check=True)
                        last.then_inc(blocks, 1)
                        for r in pairs(s, LOOK, at):
                            look_up(r, n, rp, hg, at)
                        for r in pairs(s, WEIGH, at):
                            weigh(r, n)
                        for r in pairs(s, SUM, at):
                            if r == 0 and at == "dst":
                                pe.wait_ge(added, rp)
                                clear_sums()
                            add_up(r, n)
                steps(pe, body)
                n = N_HG * N_RP
                for s in range(SUM):
                    if s < LOOK:
                        look_up(NB + s - LOOK, (N_RP - 1) * N_HG, N_RP - 1, 0, "src")
                    if s < WEIGH:
                        weigh(s - WEIGH, n)
                    add_up(s - SUM, n)

            @blk.vector
            def _(dve):
                dve.sem_inc(msgs, B_MSGS)
                dve.sem_inc(split, B_SPLIT)
                dve.wait_ge(cleared, 1)

                def message_steps(r, n):
                    u, h, k = r % 2, (r % NP) // HP, r % HP
                    i = (n * NP + r) * 3
                    q_e = ps_l[u][:, 4 * D:6 * D].rearrange("p (t d) -> p t d", t=2)
                    kv_e = ps_l[u][:, 0:4 * D].rearrange("p (t a d) -> p t a d", t=2, a=2)
                    dve.wait_ge(looked, n * NP + (r + 1 + B_LOOKED))
                    if not (isinstance(i, int) and i == 0):
                        dve.wait_ge(step, i)
                    dve.tensor_tensor(qw[:], q_e, edges[h][:, :, k, 0:D], ALU.mult).then_inc(step, 1)
                    yield
                    dve.wait_ge(step, i + 1)
                    dve.tensor_tensor(qwk[:], kv_e[:, :, 0], qw[:], ALU.mult).then_inc(step, 1)
                    yield
                    dve.wait_ge(step, i + 2)
                    dve.wait_ge(msgs, n * NP + (r + B_MSGS))
                    dve.tensor_reduce(alpha[:], qwk[:].rearrange("p t (a c) -> p (t a) c", c=8), AX.X, ALU.add)\
                       .then_inc(step, 1)
                    yield
                    dve.wait_ge(step, i + 3)
                    dve.wait_ge(split, n * NP + (r + 1))
                    dve.tensor_tensor(msg[r % 5][:].rearrange("p t (a c) -> p t a c", c=8),
                                      kv_e[:, :, 1].rearrange("p t (a c) -> p t a c", c=8),
                                      alpha[:].rearrange("p (t a) -> p t a", t=2).unsqueeze(3)
                                      .to_broadcast([128, 2, 8, 8]), ALU.mult).then_inc(msgs, 1)
                    yield

                def first_rest(r, n):
                    dve.wait_ge(part0, n * NP + (r + 1))
                    dve.tensor_tensor(rest[r % 5][:], msg[r % 5][:], parts[r % NP][:, :, 0:D], ALU.subtract)\
                       .then_inc(rests, 1)

                def part_2(r, n):
                    dve.wait_ge(part1, n * NP + (r + 1))
                    dve.tensor_tensor(parts[r % NP][:, :, 2 * D:3 * D], rest[r % 5][:], parts[r % NP][:, :, D:2 * D],
                                      ALU.subtract).then_inc(split, 1)

                def one_hots(s, t):
                    lanes = edges[s // HP][:, t, s % HP, DST_LANE:DST_LANE + 2]
                    return dve.tensor_tensor(hot[s][:, t], iota1[:].unsqueeze(1).to_broadcast([128, 2, 128]),
                                             lanes.unsqueeze(2).to_broadcast([128, 2, 128]), ALU.is_equal)

                def add_sums(rp, n):
                    dve.wait_ge(summed, n * NP + B_SUMMED)
                    d0 = bass.ds(2 * rp, 2) if not isinstance(rp, int) else slice(2 * rp, 2 * rp + 2)
                    at = acc[:, d0, :].rearrange("p h c -> p (h c)")
                    dve.tensor_copy(at, ps_o[0:NL, 0:2 * MW]).then_inc(added, 1)

                def messages_of(s, at, n):
                    return [message_steps(r, n) for r in pairs(s, MESSAGE, at)]

                def body(rp, hg, n, at):
                    for s in range(NP):
                        if s % HP == 0:
                            dve.wait_ge(loaded[s // HP], 16 * n + 16)
                        dve.wait_ge(summed, n * NP + (s + 1))
                        if s == SUM and at == "dst":
                            add_sums(rp - 1, n)
                        one_hots(s, 0)
                        chain = messages_of(s, at, n)
                        for c in chain:
                            next(c)
                        one_hots(s, 1).then_inc(hots, 1)
                        for c in chain:
                            next(c)
                        for r in pairs(s, REST, at):
                            first_rest(r, n)
                        for c in chain:
                            next(c)
                        for r in pairs(s, PART2, at):
                            part_2(r, n)
                        for c in chain:
                            next(c)
                steps(dve, body)
                n = N_HG * N_RP
                for s in range(SUM):
                    if s < MESSAGE:
                        for _ in message_steps(s - MESSAGE, n):
                            pass
                    if s < REST:
                        first_rest(s - REST, n)
                    if s < PART2:
                        part_2(s - PART2, n)
                add_sums(N_RP - 1, n)


YB = NB + 1


def spill_messages(nc, io, sorted_rows, qkv_rows, y_rows, y_sb, n_spilled, ident):
    W = D + 2
    with ExitStack() as ctx:
        sb = lambda name, shape, dt: ctx.enter_context(nc.sbuf_tensor(f"spill_{name}", shape, dt))
        pb = lambda name, shape, dt=F32: ctx.enter_context(nc.psum_tensor(f"spill_{name}", shape, dt))
        sem = ctx.enter_context(Semaphores(nc))
        edges = sb("edges", [TE, ROW], F32)
        before = sb("before", [TE, TE], F32)
        lane_col = sb("lane_col", [TE, 1], F32)
        zeros = sb("zeros", [TE, YB * W], F32)
        dst_at, src_at, to = sb("dst_at", [TE, 1], I32), sb("src_at", [TE, 1], I32), sb("to", [TE, 1], I32)
        of_dst, of_src = sb("of_dst", [TE, 3 * D], F32), sb("of_src", [TE, 3 * D], F32)
        same, earlier = sb("same", [TE, TE], F32), sb("earlier", [TE, TE], F32)
        seen, spare = sb("seen", [TE, 1], F32), sb("spare", [TE, 1], F32)
        qw, alpha = sb("qw", [TE, D], F32), sb("alpha", [TE, 8], F32)
        msg = sb("msg", [TE, W], F32)
        total = sb("total", [TE, W], F32)
        ps_id, ps_sum = pb("ps_id", [128, 512]), pb("ps_sum", [128, 512])
        const, cleared, loaded, ids = (sem(n) for n in ("const", "cleared", "loaded", "ids"))
        row_ids, matched, summed, ready = (sem(n) for n in ("row_ids", "matched", "summed", "ready"))
        rows, added = sem.of_pool_dma("spill_rows"), sem.of_pool_dma("spill_added")
        step, taken, y_in = sem("step"), sem("taken"), sem("y_in")
        with nc.Block() as blk:
            @blk.sync
            def _(sp):
                n = sp.value_load(n_spilled[0:1, 0:1], min_val=1, max_val=NT + 1)
                sp.dma_start(before[:], io["tri"][0:TE, 0:TE]).then_inc(const, 16)
                sp.dma_start(lane_col[:], io["lanes"][0:TE, :]).then_inc(const, 16)
                sp.wait_ge(cleared, 1)
                sp.dma_start(y_rows.rearrange("(p b) c -> p (b c)", b=YB), zeros[:]).then_inc(const, 16)
                with sp.Fori(0, n) as t:
                    sp.wait_ge(added, 16 * t)
                    sp.sem_inc(taken, 1)
                    sp.dma_start(edges[:], sorted_rows[bass.ds(N_SLOTS + t * TE, TE), :]).then_inc(loaded, 16)
                sp.wait_ge(added, 16 * n)
                sp.sem_inc(taken, 1)
                sp.dma_start(y_sb, y_rows[0:N_NODES, :].rearrange("(p b) c -> p (b c)", b=NB)).then_inc(y_in, 16)
                sp.wait_ge(y_in, 16)

            @blk.gpsimd
            def _(pool):
                n = pool.value_load(n_spilled[0:1, 0:1], min_val=1, max_val=NT + 1)
                pool.memset(zeros[:], 0.0).then_inc(cleared, 1)
                pool.wait_ge(const, 48)
                with pool.Fori(0, n) as t:
                    pool.wait_ge(ids, t + 1)
                    pool.sem_inc(taken, 1)
                    pool.indirect_dma_start(out=of_dst[:], out_offset=None, in_=qkv_rows,
                                            in_offset=bass.IndirectOffsetOnAxis(dst_at[:, 0:1], 0)).then_inc(rows, 16)
                    pool.indirect_dma_start(out=of_src[:], out_offset=None, in_=qkv_rows,
                                            in_offset=bass.IndirectOffsetOnAxis(src_at[:, 0:1], 0)).then_inc(rows, 16)
                    pool.wait_ge(ready, t + 1)
                    pool.sem_inc(taken, 1)
                    pool.indirect_dma_start(out=y_rows, out_offset=bass.IndirectOffsetOnAxis(to[:, 0:1], 0),
                                            in_=total[:], in_offset=None, compute_op=ALU.add).then_inc(added, 16)
                    pool.wait_ge(added, 16 * t + 16)

            @blk.tensor
            def _(pe):
                n = pe.value_load(n_spilled[0:1, 0:1], min_val=1, max_val=NT + 1)
                with pe.Fori(0, n) as t:
                    pe.wait_ge(loaded, 16 * t + 16)
                    nc.tensor.matmul(ps_id[0:TE, 0:TE], edges[:, DST:DST + 1].to_broadcast([TE, TE]),
                                     ident[0:TE, 0:TE], start=True, stop=True).then_inc(row_ids, 1)
                    pe.wait_ge(matched, t + 1)
                    nc.tensor.matmul(ps_sum[0:TE, 0:W], same[:], msg[:], start=True, stop=True).then_inc(summed, 1)

            @blk.vector
            def _(dve):
                n = dve.value_load(n_spilled[0:1, 0:1], min_val=1, max_val=NT + 1)
                dve.wait_ge(const, 48)
                with dve.Fori(0, n) as t:
                    k = [0]

                    def link(ins):
                        k[0] += 1
                        ins.then_inc(step, 1)
                        dve.wait_ge(step, t * 9 + k[0])

                    dve.wait_ge(loaded, 16 * t + 16)
                    dve.tensor_copy(dst_at[:], edges[:, DST:DST + 1])
                    dve.tensor_copy(src_at[:], edges[:, SRC:SRC + 1]).then_inc(ids, 1)
                    dve.wait_ge(row_ids, t + 1)
                    link(dve.tensor_scalar(same[:], ps_id[0:TE, 0:TE], edges[:, DST:DST + 1], None, ALU.is_equal))
                    link(dve.tensor_tensor(earlier[:], same[:], before[:], ALU.mult))
                    link(dve.tensor_reduce(seen[:], earlier[:], AX.X, ALU.max))
                    link(dve.scalar_tensor_tensor(spare[:], lane_col[:], float(N_NODES), edges[:, DST:DST + 1],
                                                  ALU.add, ALU.subtract))
                    link(dve.tensor_tensor(spare[:], spare[:], seen[:], ALU.mult))
                    dve.tensor_tensor(to[:], spare[:], edges[:, DST:DST + 1], ALU.add)
                    dve.wait_ge(rows, 32 * t + 32)
                    link(dve.tensor_tensor(qw[:], of_dst[:, 0:D], edges[:, 0:D], ALU.mult))
                    link(dve.tensor_tensor(qw[:], qw[:], of_src[:, D:2 * D], ALU.mult))
                    link(dve.tensor_reduce(alpha[:], qw[:].rearrange("p (a c) -> p a c", c=8), AX.X, ALU.add))
                    dve.tensor_tensor(msg[:, 0:D].rearrange("p (a c) -> p a c", c=8),
                                      of_src[:, 2 * D:3 * D].rearrange("p (a c) -> p a c", c=8),
                                      alpha[:].unsqueeze(2).to_broadcast([TE, 8, 8]), ALU.mult)
                    dve.tensor_copy(msg[:, D + 1:W], edges[:, ONE:ONE + 1])
                    link(dve.tensor_reduce(msg[:, D:D + 1], edges[:, W1:W1 + 3], AX.X, ALU.add))
                    dve.sem_inc(matched, 1)
                    dve.wait_ge(summed, t + 1)
                    dve.tensor_copy(total[:], ps_sum[0:TE, 0:W]).then_inc(ready, 1)
                    dve.wait_ge(ready, t + 1)
                    assert k[0] == 9


def collect(nc, acc, y_sb, node_sums):
    W = D + 2
    y3 = y_sb.rearrange("p (b c) -> p b c", c=W)
    with ExitStack() as ctx:
        step = ctx.enter_context(Semaphores(nc))("step")
        with nc.Block() as blk:
            @blk.vector
            def _(dve):
                n = [0]

                def link(ins):
                    n[0] += 1
                    ins.then_inc(step, 1)
                    dve.wait_ge(step, n[0])
                for i in range(3):
                    link(dve.tensor_tensor(y3[:, :, 0:D], y3[:, :, 0:D], acc[:, :, i * D:(i + 1) * D], ALU.add))
                    link(dve.tensor_tensor(y3[:, :, D:D + 1], y3[:, :, D:D + 1], acc[:, :, 3 * D + i:3 * D + i + 1],
                                           ALU.add))
                link(dve.tensor_tensor(y3[:, :, D + 1:W], y3[:, :, D + 1:W], acc[:, :, MW - 1:MW], ALU.add))
                dve.tensor_copy(node_sums[:], y3)


def scale_of_degree(nc, tag, degree, extra, dinv):
    with ExitStack() as ctx:
        step = ctx.enter_context(Semaphores(nc))("step")
        with nc.Block() as blk:
            @blk.vector
            def _(dve):
                dve.tensor_scalar(dinv[:], degree, extra, 1e-12, ALU.add, ALU.max).then_inc(step, 1)
                dve.wait_ge(step, 2)
                dve.reciprocal(dinv[:], dinv[:])

            @blk.scalar
            def _(act):
                act.wait_ge(step, 1)
                act.activation(dinv[:], dinv[:], ACT.Sqrt).then_inc(step, 1)


def layer_norm(nc, tag, x, add, scale, tmp, out=None, out_rows=None):
    with ExitStack() as ctx:
        sb = lambda name, shape, dt: ctx.enter_context(nc.sbuf_tensor(f"{tag}_{name}", shape, dt))
        step = ctx.enter_context(Semaphores(nc))("step")
        rooted = ctx.enter_context(Semaphores(nc))("rooted")
        stored = ctx.enter_context(Semaphores(nc))("ln_stored")
        mean, var = sb("mean", [NL, NB], F32), sb("var", [NL, NB], F32)
        wide = lambda a: a[:].unsqueeze(2).to_broadcast([NL, NB, D])
        with nc.Block() as blk:
            @blk.vector
            def _(dve):
                n = [0]

                def link(ins):
                    n[0] += 1
                    ins.then_inc(step, 1)
                    dve.wait_ge(step, n[0])
                link(dve.scalar_tensor_tensor(x[:], add, scale, x[:], ALU.mult, ALU.add))
                link(dve.tensor_reduce(mean[:], x[:], AX.X, ALU.add))
                link(dve.tensor_scalar(mean[:], mean[:], 1.0 / D, None, ALU.mult))
                link(dve.tensor_tensor(x[:], x[:], wide(mean), ALU.subtract))
                link(dve.tensor_tensor(tmp[:], x[:], x[:], ALU.mult))
                link(dve.tensor_reduce(var[:], tmp[:], AX.X, ALU.add))
                link(dve.tensor_scalar(var[:], var[:], 1.0 / D, 1e-5, ALU.mult, ALU.add))
                dve.wait_ge(rooted, 1)
                link(dve.reciprocal(var[:], var[:]))
                link(dve.tensor_tensor(x[:], x[:], wide(var), ALU.mult))

            @blk.scalar
            def _(act):
                act.wait_ge(step, 7)
                act.activation(var[:], var[:], ACT.Sqrt).then_inc(rooted, 1)

            if out_rows is not None:
                @blk.sync
                def _(sp):
                    sp.wait_ge(step, 9)
                    sp.dma_start(out_rows.rearrange("(p b) d -> p b d", b=NB), x[:]).then_inc(stored, 16)
                    sp.wait_ge(stored, 16)


def spread(nc, tag, n_passes, matrix, exact, use_weight, gather, scatter, io, sorted_rows, rows, y_rows, n_spilled,
           ident, xs, parts, sums, y_sb, post_vector, post_scalar, before_vector=None):
    MC = matrix.shape[3]
    HR = NB // 2
    CHUNK = 10
    N_CHUNKS = NB // CHUNK
    AHEAD = 2
    N2 = 24
    DVE_S = 15
    with ExitStack() as ctx:
        sb = lambda name, shape, dt: ctx.enter_context(nc.sbuf_tensor(f"{tag}_{name}", shape, dt))
        pb = lambda name, shape, dt=F32: ctx.enter_context(nc.psum_tensor(f"{tag}_{name}", shape, dt))
        sem = ctx.enter_context(Semaphores(nc))
        two = range(2)
        if exact:
            chunk = [sb(f"chunk{c}", [128, CHUNK, MC], F32) for c in range(N_CHUNKS)]
            third = [[sb(f"third{c}{i}", [128, CHUNK, 128], BF16) for i in range(3)] for c in range(N_CHUNKS)]
        else:
            mat = [[sb(f"mat{u}{h}", [128, HR, MC], matrix.dtype) for h in two] for u in two]
            cast = [[sb(f"cast{u}{h}", [128, HR, MC], BF16) for h in two] for u in two]
        ps = [pb(f"ps{u}", [128, 512]) for u in two]
        edges = sb("edges", [TE, ROW], F32)
        before = sb("before", [TE, TE], F32)
        lane_col = sb("lane_col", [TE, 1], F32)
        zeros = sb("zeros", [TE, YB * D], F32)
        from_at, to = sb("from_at", [TE, 1], I32), sb("to", [TE, 1], I32)
        of_node = sb("of_node", [TE, D], F32)
        same, earlier = sb("same", [TE, TE], F32), sb("earlier", [TE, TE], F32)
        seen, spare, factor = sb("seen", [TE, 1], F32), sb("spare", [TE, 1], F32), sb("factor", [TE, 1], F32)
        msg, total = sb("msg", [TE, D], F32), sb("total", [TE, D], F32)
        ps_id, ps_sum = pb("ps_id", [128, 512]), pb("ps_sum", [128, 512])
        loaded = [[sem(f"mat_loaded{u}{h}") for h in two] for u in two]
        const, cleared, xs_ready, table = sem("const"), sem("cleared"), sem("xs_ready"), sem("table")
        got, ids, fetched, row_ids, matched = sem("got"), sem("ids"), sem.of_pool_dma(f"{tag}_fetched"), sem("row_ids"), sem("matched")
        summed, ready, added, y_in = sem("summed"), sem("ready"), sem.of_pool_dma(f"{tag}_added"), sem("y_in")
        row_done, row_kept, step, taken = sem("row_done"), sem("row_kept"), sem("step"), sem("taken")
        cast_v, cast_a = sem("cast_v"), sem("cast_a")
        chunk_in = [sem(f"chunk_in{c}") for c in range(N_CHUNKS)]
        first_out, rest_out, second_out, third_out = (sem(n) for n in ("first_out", "rest_out", "second_out", "third_out"))
        chunk_done, pads = sem("chunk_done"), sem("pads")
        B_ROW, B_THIRD, B_DONE = 2, 1, N_CHUNKS

        def splits(step, k, r2):
            for u in two:
                yield u, [(lambda j=j: step((k * NB + 2 * r2 + u) * N_CHUNKS + (AHEAD + j), (AHEAD + j) % N_CHUNKS,
                                            u + (AHEAD + j) // N_CHUNKS)) for j in range(N_CHUNKS)]
        post = {n: sem(n) for n in ("post_v", "post_s")}

        passes = lambda e: e.Fori(0, n_passes) if n_passes > 1 else nullcontext(0)
        count = lambda e: e.value_load(n_spilled[0:1, 0:1], min_val=1, max_val=NT + 1)
        with nc.Block() as blk:
            @blk.sync
            def _(sp):
                n = count(sp)
                sp.dma_start(before[:], io["tri"][0:TE, 0:TE]).then_inc(const, 16)
                sp.dma_start(lane_col[:], io["lanes"][0:TE, :]).then_inc(const, 16)
                sp.wait_ge(cleared, 1)
                with passes(sp) as k:
                    sp.wait_ge(xs_ready, k + 1)
                    sp.sem_inc(taken, 1)
                    sp.dma_start(rows.rearrange("(p b) d -> p (b d)", b=NB),
                                 xs[:].rearrange("p b d -> p (b d)")).then_inc(table, 16)
                    sp.dma_start(y_rows.rearrange("(p b) c -> p (b c)", b=YB), zeros[:]).then_inc(table, 16)
                    with sp.Fori(0, n) as t:
                        sp.wait_ge(added, (k * n + t) * 16)
                        sp.sem_inc(taken, 1)
                        sp.dma_start(edges[:], sorted_rows[bass.ds(N_SLOTS + t * TE, TE), :]).then_inc(got, 16)
                    sp.wait_ge(added, (k * n + n) * 16)
                    sp.sem_inc(taken, 1)
                    sp.dma_start(y_sb[:].rearrange("p b d -> p (b d)"),
                                 y_rows[0:N_NODES, :].rearrange("(p b) c -> p (b c)", b=NB)).then_inc(y_in, 16)
                sp.wait_ge(y_in, 16 * n_passes)

            @blk.gpsimd
            def _(pool):
                n = count(pool)
                pool.memset(zeros[:], 0.0).then_inc(cleared, 1)
                if exact:
                    for c in range(N_CHUNKS):
                        for i in range(3):
                            last = pool.memset(third[c][i][:, :, MC:128], 0.0)
                    last.then_inc(pads, 1)
                with passes(pool) as k:
                    pool.wait_ge(table, 32 * k + 32)
                    pool.sem_inc(taken, 1)
                    with pool.Fori(0, n) as t:
                        pool.wait_ge(ids, k * n + t + 1)
                        pool.sem_inc(taken, 1)
                        pool.indirect_dma_start(out=of_node[:], out_offset=None, in_=rows,
                                                in_offset=bass.IndirectOffsetOnAxis(from_at[:, 0:1], 0))\
                            .then_inc(fetched, 16)
                        pool.wait_ge(ready, k * n + t + 1)
                        pool.sem_inc(taken, 1)
                        pool.indirect_dma_start(out=y_rows, out_offset=bass.IndirectOffsetOnAxis(to[:, 0:1], 0),
                                                in_=total[:], in_offset=None, compute_op=ALU.add).then_inc(added, 16)
                        pool.wait_ge(added, (k * n + t) * 16 + 16)

            @blk.scalar
            def _(act):
                def load(r, u):
                    for h in two:
                        src = matrix[bass.ds(r, 1), :, h * HR:(h + 1) * HR, :] if not isinstance(r, int) else \
                            matrix[r:r + 1, :, h * HR:(h + 1) * HR, :]
                        act.dma_start(mat[u][h][:].rearrange("p s d -> p (s d)"),
                                      src.rearrange("a p s d -> (a p) (s d)")).then_inc(loaded[u][h], 16)

                def load_chunk(row, c):
                    row = bass.ds(row, 1) if not isinstance(row, int) else slice(row % NB, row % NB + 1)
                    act.dma_start(chunk[c][:].rearrange("p s d -> p (s d)"),
                                  matrix[row, :, c * CHUNK:(c + 1) * CHUNK, :].rearrange("a p s d -> (a p) (s d)"))\
                       .then_inc(chunk_in[c], 16)

                def first_part(number, row_16, c):
                    act.wait_ge(chunk_in[c], row_16)
                    act.wait_ge(chunk_done, number + 1)
                    act.activation(third[c][0][:, :, 0:MC], chunk[c][:], ACT.Copy).then_inc(first_out, 1)

                def split_rows(k, r2):
                    def step(number, c, ahead):
                        row = k * NB + 2 * r2 + ahead
                        nxt = (c + 1) % N_CHUNKS
                        first_part(number + 1, (row + (1 if nxt == 0 else 0)) * 16 + 16, nxt)
                        act.wait_ge(rest_out, number + 1)
                        act.activation(third[c][1][:, :, 0:MC], chunk[c][:], ACT.Copy).then_inc(second_out, 1)
                        act.wait_ge(second_out, number + 1)
                        act.wait_ge(third_out, number + B_THIRD)
                        load_chunk(2 * r2 + (ahead + (1 if c > 0 else 0)), (c - 1) % N_CHUNKS)
                    return step

                def exact_rows(k, r2):
                    for u, steps in splits(split_rows(k, r2), k, r2):
                        for go in steps:
                            go()

                if exact:
                    for c in range(N_CHUNKS - 1):
                        load_chunk(0, c)
                    first_part(0, 16, 0)
                    for c in range(AHEAD):
                        split_rows(0, 0)(c, c, 0)
                    with passes(act) as k:
                        with act.Fori(0, N2) as r2:
                            exact_rows(k, r2)
                        exact_rows(k, N2)
                        post_scalar(act, k, post)
                    for c in range(N_CHUNKS):
                        act.wait_ge(chunk_in[c], 16 * (NB * n_passes + (2 if c == 0 else 1)))
                    return

                def done_with(k, r2, u):
                    act.wait_ge(row_done, k * NB + 2 * r2 + (u + B_ROW - 1))
                    for h in two:
                        act.wait_ge(loaded[u][h], (k * (NB // 2) + r2) * 16 + 16)
                        act.activation(cast[u][h][:, DVE_S:HR, :], mat[u][h][:, DVE_S:HR, :], ACT.Copy)\
                           .then_inc(cast_a, 1)
                    act.wait_ge(cast_a, (k * NB + 2 * r2 + u) * 2 + 2)
                    act.wait_ge(cast_v, (k * NB + 2 * r2 + u) * 2 + 2)

                for u in two:
                    load(u, u)
                with passes(act) as k:
                    with act.Fori(0, N2) as r2:
                        for u in two:
                            done_with(k, r2, u)
                            load(2 * r2 + (2 + u), u)
                    for u in two:
                        done_with(k, N2, u)
                        load(u, u)
                    post_scalar(act, k, post)
                for u in two:
                    for h in two:
                        act.wait_ge(loaded[u][h], 16 * (NB // 2 * n_passes + 1))

            @blk.tensor
            def _(pe):
                n = count(pe)
                pe.sem_inc(row_done, B_ROW)
                if exact:
                    pe.sem_inc(chunk_done, B_DONE)
                    pe.wait_ge(pads, 1)
                with passes(pe) as k:
                    def dst_rows(r2):
                        for u in two:
                            r = 2 * r2 + u
                            pe.wait_ge(row_kept, k * NB + r)
                            if exact:
                                for c in range(N_CHUNKS):
                                    pe.wait_ge(third_out, (k * NB + r) * N_CHUNKS + (c + 1 + B_THIRD))
                                    for b in range(c * CHUNK, (c + 1) * CHUNK):
                                        for i in range(3):
                                            last = nc.tensor.matmul(ps[u][:, 0:3 * D],
                                                                    third[c][i][0:NL, b - c * CHUNK, :],
                                                                    parts[:, b].rearrange("p i d -> p (i d)"),
                                                                    start=b == 0 and i == 0,
                                                                    stop=b == NB - 1 and i == 2)
                                    if c < N_CHUNKS - 1:
                                        last.then_inc(chunk_done, 1)
                                last.then_inc(row_done, 1)
                                pe.wait_ge(row_done, k * NB + r + (1 + B_ROW))
                                pe.sem_inc(chunk_done, 1)
                                continue
                            for h in two:
                                for by in (cast_a, cast_v):
                                    pe.wait_ge(by, (k * NB + r) * 2 + (h + 1))
                                for s in range(HR):
                                    b = h * HR + s
                                    last = nc.tensor.matmul(ps[u][:, 0:3 * D], cast[u][h][0:NL, s, :],
                                                            parts[:, b].rearrange("p i d -> p (i d)"),
                                                            start=b == 0, stop=b == NB - 1)
                            last.then_inc(row_done, 1)

                    pe.wait_ge(xs_ready, k + 1)
                    pe.sem_inc(taken, 1)
                    with pe.Fori(0, N2 // 2) as r2:
                        dst_rows(r2)
                    with pe.Fori(0, n) as t:
                        pe.wait_ge(got, (k * n + t) * 16 + 16)
                        nc.tensor.matmul(ps_id[0:TE, 0:TE], edges[:, scatter:scatter + 1].to_broadcast([TE, TE]),
                                         ident[0:TE, 0:TE], start=True, stop=True).then_inc(row_ids, 1)
                        pe.wait_ge(matched, k * n + t + 1)
                        nc.tensor.matmul(ps_sum[0:TE, 0:D], same[:], msg[:], start=True, stop=True).then_inc(summed, 1)
                    with pe.Fori(N2 // 2, N2 + 1) as r2:
                        dst_rows(r2)

            @blk.vector
            def _(dve):
                n = count(dve)
                dve.wait_ge(const, 32)
                if before_vector is not None:
                    before_vector(dve)
                dve.sem_inc(xs_ready, 1)
                dve.sem_inc(row_kept, 1)

                def turn(k, r2, u):
                    dve.wait_ge(row_done, k * NB + 2 * r2 + (u + B_ROW - 1))
                    for h in two:
                        dve.wait_ge(loaded[u][h], (k * (NB // 2) + r2) * 16 + 16)
                        dve.tensor_copy(cast[u][h][:, 0:DVE_S, :], mat[u][h][:, 0:DVE_S, :]).then_inc(cast_v, 1)

                def take_rest(number, c):
                    dve.wait_ge(first_out, number + 1)
                    dve.tensor_tensor(chunk[c][:], chunk[c][:], third[c][0][:, :, 0:MC], ALU.subtract)\
                       .then_inc(rest_out, 1)

                def split_step(number, c, ahead):
                    take_rest(number + 1, (c + 1) % N_CHUNKS)
                    dve.wait_ge(rest_out, number + 1)
                    dve.wait_ge(second_out, number + 1)
                    dve.tensor_tensor(third[c][2][:, :, 0:MC], chunk[c][:], third[c][1][:, :, 0:MC], ALU.subtract)\
                       .then_inc(third_out, 1)

                if exact:
                    dve.sem_inc(third_out, B_THIRD)
                    take_rest(0, 0)
                    for c in range(AHEAD):
                        split_step(c, c, 0)
                else:
                    turn(0, 0, 0)
                with passes(dve) as k:
                    def keep_rows(r2):
                        for u, steps in splits(split_step, k, r2):
                            if exact:
                                for go in steps:
                                    go()
                            else:
                                turn(k, r2 + u, 1 - u)
                            dve.wait_ge(row_done, k * NB + (2 * r2 + (u + 1 + B_ROW)))
                            dve.tensor_reduce(sums[:, bass.ds(2 * r2 + u, 1), :].rearrange("p a d -> p (a d)"),
                                              ps[u][0:NL, 0:3 * D].rearrange("p (i d) -> p d i", i=3),
                                              AX.X, ALU.add).then_inc(row_kept, 1)

                    with dve.Fori(0, N2 // 2) as r2:
                        keep_rows(r2)
                    with dve.Fori(0, n) as t:
                        m = k * n + t
                        i = [0]

                        def link(ins):
                            i[0] += 1
                            ins.then_inc(step, 1)
                            dve.wait_ge(step, m * 7 + i[0])
                        dve.wait_ge(got, m * 16 + 16)
                        dve.tensor_copy(from_at[:], edges[:, gather:gather + 1]).then_inc(ids, 1)
                        if use_weight:
                            link(dve.tensor_reduce(factor[:], edges[:, W1:W1 + 3], AX.X, ALU.add))
                        else:
                            link(dve.tensor_copy(factor[:], edges[:, ONE:ONE + 1]))
                        id_col = edges[:, scatter:scatter + 1]
                        dve.wait_ge(row_ids, m + 1)
                        link(dve.tensor_scalar(same[:], ps_id[0:TE, 0:TE], id_col, None, ALU.is_equal))
                        link(dve.tensor_tensor(earlier[:], same[:], before[:], ALU.mult))
                        link(dve.tensor_reduce(seen[:], earlier[:], AX.X, ALU.max))
                        link(dve.scalar_tensor_tensor(spare[:], lane_col[:], float(N_NODES), id_col, ALU.add,
                                                      ALU.subtract))
                        link(dve.tensor_tensor(spare[:], spare[:], seen[:], ALU.mult))
                        dve.tensor_tensor(to[:], spare[:], id_col, ALU.add)
                        dve.wait_ge(fetched, m * 16 + 16)
                        link(dve.tensor_scalar(msg[:], of_node[:], factor[:, 0:1], None, ALU.mult))
                        dve.sem_inc(matched, 1)
                        dve.wait_ge(summed, m + 1)
                        dve.tensor_copy(total[:], ps_sum[0:TE, 0:D]).then_inc(ready, 1)
                        dve.wait_ge(ready, m + 1)
                        assert i[0] == 7
                    with dve.Fori(N2 // 2, N2 + 1) as r2:
                        keep_rows(r2)
                    dve.wait_ge(row_kept, k * NB + (NB + 1))
                    dve.wait_ge(y_in, 16 * k + 16)
                    post_vector(dve, k, post)
                    dve.sem_inc(xs_ready, 1)


class Chain:

    def __init__(self, eng, sem, k, size):
        self.eng, self.sem, self.k, self.size, self.n = eng, sem, k, size, 0

    def __call__(self, ins):
        self.n += 1
        ins.then_inc(self.sem, 1)
        self.eng.wait_ge(self.sem, self.k * self.size + self.n if self.size else self.n)


def to_parts(link, dve, parts, whole, rest):
    link(dve.tensor_copy(parts[:, :, 0, :], whole[:]))
    link(dve.tensor_tensor(rest[:], whole[:], parts[:, :, 0, :], ALU.subtract))
    link(dve.tensor_copy(parts[:, :, 1, :], rest[:]))
    link(dve.tensor_tensor(parts[:, :, 2, :], rest[:], parts[:, :, 1, :], ALU.subtract))


def wide(col):
    return col[:].unsqueeze(2).to_broadcast([NL, NB, D])


def smooth(nc, shared, x, hh, dinv, xs, parts, sums, y_sb, z, weighted):
    LAM = 0.1
    GAMMA = 1.0 / (2.0 * (1.0 - LAM))
    with ExitStack() as ctx:
        norm = ctx.enter_context(nc.sbuf_tensor("prox_norm", [NL, NB], F32))
        shrink = ctx.enter_context(nc.sbuf_tensor("prox_shrink", [NL, NB], F32))
        first = ctx.enter_context(Semaphores(nc))("first")

        def before_vector(dve):
            link = Chain(dve, first, 0, 0)
            link(dve.tensor_copy(hh[:], x[:]))
            link(dve.tensor_tensor(xs[:], x[:], wide(dinv), ALU.mult))
            to_parts(link, dve, parts, xs, z)

        def post_vector(dve, k, post):
            link = Chain(dve, post["post_v"], k, 19)
            link(dve.tensor_tensor(sums[:], sums[:], y_sb[:], ALU.add))
            link(dve.tensor_tensor(sums[:], sums[:], xs[:], ALU.add))
            link(dve.tensor_tensor(sums[:], sums[:], wide(dinv), ALU.mult))
            link(dve.tensor_tensor(sums[:], x[:], sums[:], ALU.subtract))
            link(dve.scalar_tensor_tensor(z[:], sums[:], -GAMMA * 2.0 * (1.0 - LAM), x[:], ALU.mult, ALU.add))
            link(dve.tensor_tensor(z[:], z[:], hh[:], ALU.subtract))
            link(dve.tensor_tensor(sums[:], z[:], z[:], ALU.mult))
            link(dve.tensor_reduce(norm[:], sums[:], AX.X, ALU.add))
            dve.wait_ge(post["post_s"], k + 1)
            link(dve.tensor_scalar(shrink[:], norm[:], GAMMA * LAM, 0.0, ALU.subtract, ALU.max))
            link(dve.tensor_scalar(norm[:], norm[:], 1e-12, None, ALU.max))
            link(dve.reciprocal(norm[:], norm[:]))
            link(dve.tensor_tensor(shrink[:], shrink[:], norm[:], ALU.mult))
            link(dve.tensor_tensor(z[:], z[:], wide(shrink), ALU.mult))
            link(dve.tensor_tensor(x[:], hh[:], z[:], ALU.add))
            link(dve.tensor_tensor(xs[:], x[:], wide(dinv), ALU.mult))
            to_parts(link, dve, parts, xs, z)

        def post_scalar(act, k, post):
            act.wait_ge(post["post_v"], k * 19 + 8)
            act.activation(norm[:], norm[:], ACT.Sqrt).then_inc(post["post_s"], 1)

        spread(nc, "smooth", 3, weighted, True, True, SRC, DST, *shared, xs, parts, sums, y_sb, post_vector, post_scalar,
               before_vector)


def coefficients(nc, io, x, tmp, coeff):
    P, HD2 = 6, 32
    M = N_NODES * D
    with ExitStack() as ctx:
        sb = lambda name, shape, dt=F32: ctx.enter_context(nc.sbuf_tensor(f"coeff_{name}", shape, dt))
        pb = lambda name, shape: ctx.enter_context(nc.psum_tensor(f"coeff_{name}", shape, F32))
        sem = ctx.enter_context(Semaphores(nc))
        w1, w1t, w2t = sb("w1", [HD2, D + 4]), sb("w1t", [D, HD2]), sb("w2t", [HD2, P])
        b1, b2, ones = sb("b1", [HD2, 1]), sb("b2", [NL, P]), sb("ones", [NL, NL])
        by_feature, whole, mean, sq = sb("by_feature", [NL, D]), sb("whole", [NL, 1]), sb("mean", [NL, 1]), sb("sq", [NL, 1])
        feature_mean, stats, prod = sb("feature_mean", [D, 1]), sb("stats", [HD2, 4]), sb("prod", [HD2, 4])
        h, top, e, total = sb("h", [HD2, 1]), sb("top", [NL, 1]), sb("e", [NL, P]), sb("total", [NL, 1])
        ps_f, ps_m, ps_v, ps_h = (pb(n, [128, 512]) for n in ("ps_f", "ps_m", "ps_v", "ps_h"))
        ps_c = pb("ps_c", [128, 512])
        loaded, step, product, acted, cleared = (sem(n) for n in ("loaded", "step", "product", "acted", "cleared"))
        with nc.Block() as blk:
            @blk.sync
            def _(sp):
                for dst, src in ((w1, io["L2_gnn_W1"]), (w1t, io["L2_gnn_W1_t"][0:D, :]), (w2t, io["L2_gnn_W2_t"]),
                                 (b1, io["L2_gnn_b1"].rearrange("(p a) -> p a", a=1)),
                                 (b2, io["L2_gnn_b2"].rearrange("(a n) -> a n", a=1).to_broadcast([NL, P]))):
                    sp.dma_start(dst[:], src).then_inc(loaded, 16)

            @blk.gpsimd
            def _(pool):
                pool.memset(ones[:], 1.0).then_inc(cleared, 1)

            @blk.tensor
            def _(pe):
                pe.wait_ge(loaded, 80)
                pe.wait_ge(cleared, 1)
                pe.wait_ge(step, 2)
                nc.tensor.matmul(ps_f[0:D, 0:1], by_feature[:], ones[:, 0:1], start=True, stop=True)
                nc.tensor.matmul(ps_m[0:NL, 0:1], ones[:], whole[:], start=True, stop=True).then_inc(product, 1)
                pe.wait_ge(step, 6)
                nc.tensor.matmul(ps_v[0:NL, 0:1], ones[:], sq[:], start=True, stop=True).then_inc(product, 1)
                pe.wait_ge(step, 7)
                nc.tensor.matmul(ps_h[0:HD2, 0:1], w1t[:], feature_mean[:], start=True, stop=True).then_inc(product, 1)
                pe.wait_ge(step, 14)
                nc.tensor.matmul(ps_c[0:NL, 0:P], h[:].to_broadcast([HD2, NL]), w2t[:], start=True, stop=True)\
                  .then_inc(product, 1)

            @blk.scalar
            def _(act):
                act.wait_ge(step, 10)
                act.activation(stats[:, 1:2], stats[:, 1:2], ACT.Sqrt).then_inc(acted, 1)
                act.wait_ge(step, 17)
                act.activation(e[:], e[:], ACT.Exp).then_inc(acted, 1)

            @blk.vector
            def _(dve):
                link = Chain(dve, step, 0, 0)
                link(dve.tensor_reduce(by_feature[:], x[:].rearrange("p b d -> p d b"), AX.X, ALU.add))
                link(dve.tensor_reduce(whole[:], by_feature[:], AX.X, ALU.add))
                dve.wait_ge(product, 1)
                link(dve.tensor_scalar(mean[:], ps_m[0:NL, 0:1], 1.0 / M, None, ALU.mult))
                link(dve.tensor_scalar(tmp[:], x[:], mean[:, 0:1], None, ALU.subtract))
                link(dve.tensor_tensor(tmp[:], tmp[:], tmp[:], ALU.mult))
                link(dve.tensor_reduce(sq[:], tmp[:], AX.XY, ALU.add))
                link(dve.tensor_scalar(feature_mean[:], ps_f[0:D, 0:1], 1.0 / N_NODES, None, ALU.mult))
                dve.wait_ge(loaded, 80)
                link(dve.memset(stats[:, 3:4], float(N_EDGES)))
                link(dve.tensor_copy(stats[:, 0:1], mean[0:HD2, :]))
                dve.wait_ge(product, 2)
                link(dve.tensor_scalar(stats[:, 1:2], ps_v[0:HD2, 0:1], 1.0 / (M - 1), None, ALU.mult))
                link(dve.memset(stats[:, 2:3], float(N_NODES)))
                dve.wait_ge(acted, 1)
                link(dve.tensor_tensor(prod[:], stats[:], w1[:, D:D + 4], ALU.mult))
                dve.wait_ge(product, 3)
                link(dve.tensor_reduce(h[:], prod[:], AX.X, ALU.add))
                dve.scalar_tensor_tensor(h[:], ps_h[0:HD2, 0:1], b1[:, 0:1], h[:], ALU.add, ALU.add).then_inc(cleared, 1)
                dve.wait_ge(cleared, 2)
                link(dve.tensor_scalar(h[:], h[:], 0.0, None, ALU.max))
                dve.wait_ge(product, 4)
                link(dve.tensor_tensor(e[:], ps_c[0:NL, 0:P], b2[:], ALU.add))
                link(dve.tensor_reduce(top[:], e[:], AX.X, ALU.max))
                link(dve.tensor_scalar(e[:], e[:], top[:, 0:1], None, ALU.subtract))
                dve.wait_ge(acted, 2)
                link(dve.tensor_reduce(total[:], e[:], AX.X, ALU.add))
                link(dve.reciprocal(total[:], total[:]))
                link(dve.tensor_scalar(coeff[:], e[:], total[:, 0:1], None, ALU.mult))


def polynomial(nc, shared, x, result, dis, coeff, xs, parts, sums, y_sb, rest, counts_t):
    with ExitStack() as ctx:
        first = ctx.enter_context(Semaphores(nc))("first")
        now = ctx.enter_context(nc.sbuf_tensor("coeff_now", [NL, 1], F32))

        def before_vector(dve):
            link = Chain(dve, first, 0, 0)
            link(dve.tensor_scalar(result[:], x[:], coeff[:, 0:1], None, ALU.mult))
            link(dve.tensor_tensor(xs[:], x[:], wide(dis), ALU.mult))
            to_parts(link, dve, parts, xs, rest)

        def post_vector(dve, k, post):
            link = Chain(dve, post["post_v"], k, 9)
            link(dve.tensor_tensor(sums[:], sums[:], y_sb[:], ALU.add))
            link(dve.tensor_tensor(sums[:], sums[:], wide(dis), ALU.mult))
            link(dve.tensor_copy(now[:], coeff[:, bass.ds(k + 1, 1)]))
            link(dve.scalar_tensor_tensor(result[:], sums[:], now[:, 0:1], result[:], ALU.mult, ALU.add))
            link(dve.tensor_tensor(xs[:], sums[:], wide(dis), ALU.mult))
            to_parts(link, dve, parts, xs, rest)

        spread(nc, "poly", 5, counts_t, False, False, DST, SRC, *shared, xs, parts, sums, y_sb, post_vector,
               lambda act, k, post: None, before_vector)


def convolve(nc, tag, shared, h, bias, relu, dinv, xs, parts, sums, y_sb, rest, counts):
    with ExitStack() as ctx:
        first = ctx.enter_context(Semaphores(nc))("first")

        def before_vector(dve):
            link = Chain(dve, first, 0, 0)
            link(dve.tensor_tensor(xs[:], h[:], wide(dinv), ALU.mult))
            to_parts(link, dve, parts, xs, rest)

        def post_vector(dve, k, post):
            link = Chain(dve, post["post_v"], k, 5)
            link(dve.tensor_tensor(sums[:], sums[:], y_sb[:], ALU.add))
            link(dve.tensor_tensor(sums[:], sums[:], xs[:], ALU.add))
            link(dve.tensor_tensor(sums[:], sums[:], wide(dinv), ALU.mult))
            link(dve.tensor_tensor(h[:], sums[:], bias[:].unsqueeze(1).to_broadcast([NL, NB, D]), ALU.add))
            if relu:
                link(dve.tensor_scalar(h[:], h[:], 0.0, None, ALU.max))
            else:
                link(dve.tensor_copy(sums[:], h[:]))

        spread(nc, tag, 1, counts, False, False, SRC, DST, *shared, xs, parts, sums, y_sb, post_vector,
               lambda act, k, post: None, before_vector)


def load_layer3(nc, io, w, bias):
    with ExitStack() as ctx:
        loaded = ctx.enter_context(Semaphores(nc))("w3_loaded")
        with nc.Block() as blk:
            @blk.sync
            def _(sp):
                for i in range(2):
                    sp.dma_start(w[i][:], io[f"L3_gnn_W{i + 1}"]).then_inc(loaded, 16)
                    sp.dma_start(bias[i][:], io[f"L3_gnn_b{i + 1}"].rearrange("(a n) -> a n", a=1)
                                 .to_broadcast([NL, D])).then_inc(loaded, 16)
                sp.wait_ge(loaded, 64)


def build(nc, io, out):
    dram = lambda name, shape, dt: nc.dram_tensor(name, shape, dt, kind="Internal").ap()
    key_rows = dram("key_rows", [N_EDGES], I16)
    block_rows = dram("block_rows", [N_EDGES], BF16)
    sorted_rows = dram("sorted_rows", [N_SLOTS + SPILL_ROWS, ROW], F32)
    qkv_rows = dram("qkv_rows", [N_NODES, 3 * D], F32)
    weighted = dram("weighted", [NB, 128, NB, NL], F32)
    counts = dram("counts", [NB, 128, NB, 128], U8)
    counts_t = dram("counts_t", [NB, 128, NB, 128], U8)
    Semaphores.made = {}
    with ExitStack() as ctx:
        sb = lambda name, shape, dt, c=ctx: c.enter_context(nc.sbuf_tensor(name, shape, dt))
        n_spilled = sb("n_spilled", [TE, 1], I32)
        x = sb("x", [NL, NB, D], F32)
        ident = sb("ident", [128, 128], F32)
        ident16 = sb("ident16", [128, 128], BF16)
        iota1 = sb("iota1", [128, 128], BF16)
        node_sums = sb("node_sums", [NL, NB, D + 2], F32)
        with ExitStack() as graph:
            q_parts = sb("q_parts", [NL, NB, 3, D], BF16, graph)
            kv_parts = sb("kv_parts", [NL, NB, 3, 2 * D], BF16, graph)
            with ExitStack() as sorting:
                zeroed = sorting.enter_context(Semaphores(nc))("zeroed")
                zeros = sb("zeros", [128, NB // 2 * ROW], F32, sorting)
                tbl = sb("tbl", [NL, NT, 11], F32, sorting)
                prepare(nc, io, tbl, key_rows, block_rows, sorted_rows, zeros, zeroed)
                with ExitStack() as projecting:
                    w_qkv = sb("w_qkv", [D, 3 * D], F32, projecting)
                    qkv = sb("qkv", [NL, NB, 3 * D], F32, projecting)
                    load_tables(nc, io, x, w_qkv, ident, iota1, ident16)
                    project(nc, "qkv_of", x, w_qkv[:], qkv, ident, 3 * D)
                    split_qkv(nc, qkv, q_parts, kv_parts, qkv_rows)
                sort_edges(nc, io, tbl, key_rows, block_rows, sorted_rows, zeros, zeroed, n_spilled)
            acc = sb("acc", [NL, NB, MW], F32, graph)
            build_graph(nc, io, sorted_rows, q_parts, kv_parts, iota1, ident16, acc, weighted, counts, counts_t)
            y0_rows = dram("y0_rows", [NL * YB, D + 2], F32)
            y0 = sb("y0", [NL, NB * (D + 2)], F32, graph)
            spill_messages(nc, io, sorted_rows, qkv_rows, y0_rows, y0[:], n_spilled, ident)
            collect(nc, acc, y0[:], node_sums)
        full = [sb(name, [NL, NB, D], F32) for name in ("hh", "xs", "sums", "y_sb", "rest")]
        hh, xs, sums, y_sb, rest = full
        parts = sb("parts", [NL, NB, 3, D], BF16)
        dinv1, dis2, dinv3 = (sb(name, [NL, NB], F32) for name in ("dinv1", "dis2", "dinv3"))
        coeff = sb("coeff", [NL, 6], F32)
        w3 = [sb(f"w3_{i}", [D, D], F32) for i in range(2)]
        bias3 = [sb(f"bias3_{i}", [NL, D], F32) for i in range(2)]
        rows = dram("rows", [N_NODES, D], F32)
        y_rows = dram("y_rows", [NL * YB, D], F32)
        shared = (io, sorted_rows, rows, y_rows, n_spilled, ident)

        layer_norm(nc, "ln0", x, node_sums[:, :, 0:D], 1.0 / (8.0 ** 0.5 * 32.0), rest)
        scale_of_degree(nc, "dinv1", node_sums[:, :, D], 1.0, dinv1)
        scale_of_degree(nc, "dis2", node_sums[:, :, D + 1], 0.0, dis2)
        scale_of_degree(nc, "dinv3", node_sums[:, :, D + 1], 1.0, dinv3)
        smooth(nc, shared, x, hh, dinv1, xs, parts, sums, y_sb, rest, weighted)
        layer_norm(nc, "ln1", x, hh[:], 1.0, rest)
        coefficients(nc, io, x, rest, coeff)
        polynomial(nc, shared, x, hh, dis2, coeff, xs, parts, sums, y_sb, rest, counts_t)
        layer_norm(nc, "ln2", x, hh[:], 1.0, rest)
        load_layer3(nc, io, w3, bias3)
        project(nc, "conv1_of", x, w3[0][:], hh, ident, D)
        convolve(nc, "conv1", shared, hh, bias3[0], True, dinv3, xs, parts, sums, y_sb, rest, counts)
        project(nc, "conv2_of", hh, w3[1][:], sums, ident, D)
        convolve(nc, "conv2", shared, sums, bias3[1], False, dinv3, xs, parts, hh, y_sb, rest, counts)
        layer_norm(nc, "ln3", x, sums[:], 1.0, rest, out_rows=out)


def kernel(**inputs):
    import numpy as np
    import concourse.bacc as bacc
    from concourse.bass_utils import run_bass_kernel_spmd

    a = {k.replace("L0_gnn_", ""): np.ascontiguousarray(v) for k, v in inputs.items()}
    cols = lambda v: np.ascontiguousarray(v.reshape(NT, TE).T)
    a["dst_cols"], a["src_cols"], a["weight_cols"] = cols(a["dst"]), cols(a["src"]), cols(a.pop("edge_weight"))
    a["attr16_t"] = np.ascontiguousarray(a.pop("edge_attr_16").T)
    a["attr8_t"] = np.ascontiguousarray(a.pop("edge_attr_8").T)
    a["L2_gnn_W1_t"], a["L2_gnn_W2_t"] = (np.ascontiguousarray(a[n].T) for n in ("L2_gnn_W1", "L2_gnn_W2"))
    a["iota"] = np.tile(np.arange(128, dtype=np.float32), (128, 1))
    a["lanes"] = np.arange(128, dtype=np.float32).reshape(128, 1)
    a["tri"] = np.tril(np.ones((128, 128), np.float32), -1)
    a["tri_t"] = np.triu(np.ones((128, 128), np.float32), 1)
    a["ident"] = np.eye(128, dtype=np.float32)

    nc = bacc.Bacc("TRN2", target_bir_lowering=False, num_devices=1)
    io = {n: nc.dram_tensor(f"in_{n}", v.shape, mybir.dt.from_np(v.dtype), kind="ExternalInput").ap()
          for n, v in a.items()}
    out = nc.dram_tensor("out", [N_NODES, D], F32, kind="ExternalOutput").ap()
    build(nc, io, out)
    r = run_bass_kernel_spmd(nc, [{f"in_{n}": v for n, v in a.items()}], core_ids=[0])
    return r.results[0]["out"]
```
